# Optimizing a Trainium2 kernel written in Bass

```python
import numpy as np
import jax
import jax.numpy as jnp

def _softmax(x, axis=-1):
    return jax.nn.softmax(x, axis=axis)

def _gelu(x):
    return jax.nn.gelu(x, approximate=True)

def _silu(x):
    return jax.nn.silu(x)

def _sigmoid(x):
    return jax.nn.sigmoid(x)

def _layernorm(x, axis=-1, eps=1e-05):
    m = jnp.mean(x, axis=axis, keepdims=True)
    v = jnp.var(x, axis=axis, keepdims=True)
    return (x - m) / jnp.sqrt(v + eps)

def _scatter_add(tgt, idx, src, axis=0):
    return tgt.at[idx].add(src)

def _segment_sum(src, seg, n):
    return jax.ops.segment_sum(src, seg, n)
kernel_name = 'mk_adj_resnorm_d2_adj_r2_2f37e4'

def setup_inputs(seed: int=0):
    np.random.seed(seed)
    _w = jnp.asarray

    def _rec_inputs():
        import jax
        import jax.numpy as jnp
        _gk = jax.random.key(seed)
        x = -0.001003 + 1 * jax.random.normal(jax.random.fold_in(_gk, 1), (6144, 128), jnp.float32)
        _w = (1.0 + jnp.arange(6144, dtype=jnp.float32)) ** (-0.5)
        _w = _w / _w.mean()
        _pij = jnp.clip(0.000325521 * _w[:, None] * _w[None, :], 0.0, 1.0)
        _a = jax.random.uniform(jax.random.fold_in(_gk, 2), (6144, 6144)) < _pij
        adj = _a.astype(jnp.int32)
        return (x, adj)
    x, adj = _rec_inputs()

    def _L0_gnn_setup():
        import jax, jax.numpy as jnp
        import numpy as np
        M = 6144
        N = 6144
        D = 128
        TEMPERATURE = 0.07
        NEG_PAD = jnp.float32(-2 ** 32 + 1)
        key = jax.random.key(seed)
        k1, k2, k3, k4 = jax.random.split(key, 4)
        xx_anchor = jax.random.normal(k1, (M, D), dtype=jnp.float32)
        inp = jax.random.normal(k2, (N, D), dtype=jnp.float32)
        adj = (jax.random.uniform(k3, (M, N)) < 0.002).astype(jnp.int32)
        limit = jnp.sqrt(6.0 / (D + D)).astype(jnp.float32)
        weight = jax.random.uniform(k4, (D, D), minval=-limit, maxval=limit, dtype=jnp.float32)
        return {'xx_anchor': xx_anchor, 'input': inp, 'adj': adj, 'weight': weight}
    _L0_gnn_all = _L0_gnn_setup()
    _L0_gnn_in = {k: v for k, v in _L0_gnn_all.items() if k in ('input', 'weight')}
    del _L0_gnn_all

    def _L1_gnn_setup():
        import jax, jax.numpy as jnp
        import numpy as np
        NEG_INF = -9000000000000000.0
        LEAKY_SLOPE = 0.01
        key = jax.random.key(seed)
        k1, k2, k3, k4 = jax.random.split(key, 4)
        N, F = (4096, 128)
        inp = jax.random.normal(k1, (N, F), dtype=jnp.float32)
        adj = jax.random.randint(k2, (N, N), 0, 2, dtype=jnp.int32)
        gain = 1.414
        limW = gain * np.sqrt(6.0 / (F + F))
        W = jax.random.uniform(k3, (F, F), minval=-limW, maxval=limW, dtype=jnp.float32)
        lima = gain * np.sqrt(6.0 / (2 * F + 1))
        a = jax.random.uniform(k4, (2 * F, 1), minval=-lima, maxval=lima, dtype=jnp.float32)
        return {'input': inp, 'adj': adj, 'W': W, 'a': a}
    _L1_gnn_all = _L1_gnn_setup()
    _L1_gnn_in = {k: v for k, v in _L1_gnn_all.items() if k in ('W', 'a')}
    del _L1_gnn_all
    return {'x': x, 'adj': adj, 'L0_gnn_input': _L0_gnn_in['input'], 'L0_gnn_weight': _L0_gnn_in['weight'], 'L1_gnn_W': _L1_gnn_in['W'], 'L1_gnn_a': _L1_gnn_in['a']}

def reference(x, adj, L0_gnn_input, L0_gnn_weight, L1_gnn_W, L1_gnn_a):
    import jax
    import jax.numpy as jnp

    def _L0_gnn_ref(xx_anchor, input, adj, weight):
        import jax, jax.numpy as jnp
        import numpy as np
        M = 6144
        N = 6144
        D = 128
        TEMPERATURE = 0.07
        NEG_PAD = jnp.float32(-2 ** 32 + 1)
        anchor_adj = jnp.einsum('md,de,ne->mn', xx_anchor, weight, input)
        scores = jnp.where(adj > 0, anchor_adj, NEG_PAD)
        atten = jax.nn.softmax(scores / TEMPERATURE, axis=1)
        return atten @ input

    def _L1_gnn_ref(input, adj, W, a):
        import jax, jax.numpy as jnp
        import numpy as np
        NEG_INF = -9000000000000000.0
        LEAKY_SLOPE = 0.01
        F_ = W.shape[0]
        h = input @ W
        a1, a2 = (a[:F_, 0], a[F_:, 0])
        s1 = h @ a1
        s2 = h @ a2
        e = jax.nn.leaky_relu(s1[:, None] + s2[None, :], negative_slope=LEAKY_SLOPE)
        masked = jnp.where(adj > 0, e, jnp.float32(NEG_INF))
        attention = jax.nn.softmax(masked, axis=1)
        return attention @ h
    x = _layernorm(x + _L0_gnn_ref(x, L0_gnn_input, adj, L0_gnn_weight), axis=-1)
    x = _layernorm(x + _L1_gnn_ref(x, adj, L1_gnn_W, L1_gnn_a), axis=-1)
    return x

_drawn_inputs = setup_inputs


def setup_inputs(seed=0):
    import zlib

    import numpy as np

    out = dict(_drawn_inputs(seed))
    spreads = {}
    factors = {}
    for name, (base, spread) in spreads.items():
        noise = np.random.default_rng([zlib.crc32(name.encode()), seed]).standard_normal(out[name].shape)
        drawn = base * np.exp(spread * noise) if base else spread * noise
        out[name] = jnp.asarray(drawn.astype(out[name].dtype))
    for name, factor in factors.items():
        out[name] = (out[name] * factor).astype(out[name].dtype)
    return out
```

```python
from contextlib import ExitStack

import concourse.bass as bass
from concourse import mybir

P = 128
U = 3
SUB = 3
G = SUB * P
PIECES = 6
RING = 3
ACT_COLS = 3
TEMPERATURE = 0.07
SLOPE = 0.01
EPS = 1e-5
BIG = 2.0 ** 60
HUGE = 2.0 ** 100
LEAST = -3.0e38
JSPLIT = 64

ALU = mybir.AluOpType
ACT = mybir.ActivationFunctionType
AX = mybir.AxisListType
F32 = mybir.dt.float32
BF16 = mybir.dt.bfloat16
I32 = mybir.dt.int32
U32 = mybir.dt.uint32


def graph_attention_kernel(nc, x, xT, adjT, feat, w0, w1, w1T, a, x1_dram, table, out):
    N, D = feat.shape
    NG = N // G
    C = N // P
    PC = C // PIECES
    PER_RING = PIECES // RING
    TURNS = C // U
    HW = D + 2
    WX = D + 3
    DEN = D
    COLT, ROWT = D + 1, D + 2

    mask_rows = adjT.rearrange("g j i -> (g j) i")
    scan_src = adjT.rearrange("g (p c) i -> g p c i", c=C)
    x_rows = x.rearrange("(g s p) d -> g p s d", s=SUB, p=P)
    x1_rows = x1_dram.rearrange("(g s p) d -> g p s d", s=SUB, p=P)
    out_rows = out.rearrange("(g s p) d -> g p s d", s=SUB, p=P)
    table_rows = table.rearrange("(g s p) d -> g p s d", s=SUB, p=P)
    xT_groups = xT.rearrange("d (g i) -> g d i", i=G)

    with ExitStack() as ctx:
        def sb(name, shape, dt=F32):
            return ctx.enter_context(nc.sbuf_tensor(name, shape, dt))

        def pb(name, shape, dt=F32):
            return ctx.enter_context(nc.psum_tensor(name, shape, dt))

        def sem(name):
            return ctx.enter_context(nc.semaphore(name))

        ident = sb("ident", [P, P])
        before = sb("before", [P, P])
        ones = sb("ones", [P, P])
        zrow = sb("zrow", [1, 512])
        iota_q = sb("iota_q", [P, P])
        iota_r = sb("iota_r", [P, C])
        iota_slot = sb("iota_slot", [P, C])
        iota_turn = sb("iota_turn", [1, TURNS])
        j_high = sb("j_high", [P, C])
        j_low = sb("j_low", [P, C])
        j_i = sb("j_i", [P, C], I32)
        w0_sb = sb("w0_sb", [P, D])
        w1x = sb("w1x", [P, WX])
        w1T_sb = sb("w1T_sb", [P, D])
        a_sb = sb("a_sb", [P, 2])
        mean0 = sb("mean0", [P, D])
        mean1 = sb("mean1", [P, D])
        scan_buf = sb("scan_buf", [P, RING, PC, G], I32)
        occ = sb("occ", [P, C])
        present = sb("present", [P, C])
        prefix = sb("prefix", [P, C])
        onesC = sb("onesC", [P, C])
        offs = sb("offs", [P, 2])
        pos = sb("pos", [P, C], I32)
        pos_low = sb("pos_low", [P, C], I32)
        pos_high = sb("pos_high", [P, C], I32)
        pos_round = sb("pos_round", [P, C])
        onehot_q = sb("onehot_q", [P, 2, C // PIECES * 2, P], BF16)
        onehot_r = sb("onehot_r", [P, C, C], BF16)
        j_rounds = sb("j_rounds", [P, C, 2, C], BF16)
        list_high = sb("list_high", [P, C])
        group_first = sb("group_first", [P, 1])
        lists = sb("lists", [P, NG * C, 2], I32)
        pad_bias = sb("pad_bias", [P, NG * C])
        pad_tmp = sb("pad_tmp", [P, C])
        turn_flags = sb("turn_flags", [1, TURNS])
        turn_n = sb("turn_n", [1, 1])
        turn_sum = sb("turn_sum", [1, 1])
        bounds = sb("bounds", [1, 2 * (NG + 1)], I32)
        idx = sb("idx", [P, U, 2], I32)
        st_feat = sb("st_feat", [P, U, HW])
        st_mask = sb("st_mask", [P, U, G], I32)
        kT = sb("kT", [P, U, P])
        fill = sb("fill", [P, U, G])
        stage = sb("stage", [P, U, G])
        S = sb("S", [P, C * G])
        V = sb("V", [P, C * HW])
        M = sb("M", [P, G])
        mcol = sb("mcol", [P, SUB])
        diag = sb("diag", [P, SUB, P])
        xT_sb = sb("xT_sb", [P, 2 * G])
        xres = sb("xres", [P, 2 * G])
        qT = sb("qT", [P, G])
        rden = sb("rden", [P, SUB])
        full = sb("full", [P, SUB])
        rdf = sb("rdf", [P, SUB])
        empty = sb("empty", [P, SUB])
        y = sb("y", [P, SUB, D])
        stats = sb("stats", [P, SUB, 6])
        mv = sb("mv", [P, SUB, 2])
        rstd = sb("rstd", [P, SUB])
        var = sb("var", [P, SUB])
        half = sb("half", [P, SUB], I32)
        rsq = sb("rsq", [P, SUB])
        xn = sb("xn", [P, SUB, D])
        xnT = sb("xnT", [P, G])
        xsum = sb("xsum", [P, NG])
        xmean = sb("xmean", [P, 1])
        xmean_b = sb("xmean_b", [P, P])
        hrow = sb("hrow", [P, SUB, HW])
        s1col = sb("s1col", [P, NG * SUB])

        ps_T = pb("ps_T", [P, U, P])
        ps_S = [pb(f"ps_S{u}", [P, G]) for u in range(U)]
        ps_O = pb("ps_O", [P, SUB, D + 1])
        ps_B = pb("ps_B", [P, G])
        ps_L = pb("ps_L", [P, 512])
        ps_X = pb("ps_X", [P, 512])

        s_load = sem("s_load")
        s_feat = sem("s_feat")
        s_const = sem("s_const")
        s_vconst = sem("s_vconst")
        s_wx = sem("s_wx")
        s_w1x = sem("s_w1x")
        s_mean = sem("s_mean")
        s_meanc = sem("s_meanc")
        s_xmean = sem("s_xmean")
        s_scan = [sem(f"s_scan{b}") for b in range(RING)]
        s_piece_v = sem("s_piece_v")
        s_piece_a = sem("s_piece_a")
        s_occ_free = sem("s_occ_free")
        s_tot = sem("s_tot")
        s_off = sem("s_off")
        s_hot = sem("s_hot")
        s_hot_free = sem("s_hot_free")
        s_listp = sem("s_listp")
        s_list = sem("s_list")
        s_bounds1 = sem("s_bounds1")
        s_small = sem("s_small")
        s_small_free = sem("s_small_free")
        s_apart = sem("s_apart")
        s_ones = sem("s_ones")
        s_idx = sem("s_idx")
        s_gf = [sem(f"s_gf{u}") for u in range(U)]
        s_gm = [sem(f"s_gm{u}") for u in range(U)]
        s_v = sem("s_v")
        s_tr = sem("s_tr")
        s_kt = sem("s_kt")
        s_fill = sem("s_fill")
        s_raw = sem("s_raw")
        s_sub = sem("s_sub")
        s_max = sem("s_max")
        s_mT = sem("s_mT")
        s_diag = sem("s_diag")
        s_mb = sem("s_mb")
        s_dif = sem("s_dif")
        s_p = sem("s_p")
        s_pv = sem("s_pv")
        s_pre = sem("s_pre")
        s_q = sem("s_q")
        s_O = sem("s_O")
        s_O_free = sem("s_O_free")
        s_xn = sem("s_xn")
        s_xT = sem("s_xT")
        s_xTc = sem("s_xTc")
        s_h = sem("s_h")
        s_s1 = sem("s_s1")
        s_hc = sem("s_hc")
        s_st = sem("s_st")
        s_out = sem("s_out")

        S3 = S[:, :].rearrange("p (r i) -> p r i", i=G)
        feat_all = S[:, 0:C * D]
        block = ctx.enter_context(nc.Block())

        def rounds(eng, layer, g):
            at = layer * (NG + 1)
            lo = eng.value_load(bounds[0:1, bass.ds(g + at, 1)], min_val=0, max_val=2 * NG * TURNS)
            hi = eng.value_load(bounds[0:1, bass.ds(g + at + 1, 1)], min_val=1, max_val=2 * NG * TURNS)
            return lo, hi

        def turn(eng, k, lo):
            return eng.snap(nc.s_assert_within(
                k - lo, 0, TURNS - 1, skip_runtime_bounds_check_because="a group lists at most N columns"))

        def apart(eng):
            eng.sem_inc(s_apart, 1)

        @block.sync
        def _(sp):
            sp.dma_start(w0_sb[:, :], w0).then_inc(s_load, 16)
            sp.dma_start(w1x[:, 0:D], w1).then_inc(s_load, 16)
            sp.dma_start(w1T_sb[:, :], w1T).then_inc(s_load, 16)
            sp.dma_start(a_sb[:, :], a).then_inc(s_load, 16)
            sp.dma_start(feat_all, feat.rearrange("(p c) d -> p (c d)", c=C)).then_inc(s_feat, 16)

            def scan(g):
                for n in range(PIECES):
                    b, turn = n % RING, n // RING
                    sp.wait_ge(s_piece_v, g * PIECES + n + 1)
                    sp.wait_ge(s_piece_a, g * PIECES + n + 1)
                    sp.dma_start(scan_buf[:, b, :, :],
                                 scan_src[bass.ds(g, 1), :, n * PC:(n + 1) * PC, :].rearrange("g p c i -> (g p) c i")
                                 ).then_inc(s_scan[b], 16)

            def small(layer, g):
                gg = g + layer * NG
                sp.wait_ge(s_small_free, gg + 1)
                apart(sp)
                at = bass.ds((g % 2) * G, G)
                if layer == 0:
                    sp.dma_start(xT_sb[:, at], xT_groups[bass.ds(g, 1), :, :].rearrange("g d i -> (g d) i")
                                 ).then_inc(s_small, 16)
                rows = x_rows if layer == 0 else x1_rows
                sp.dma_start(xres[:, at].rearrange("p (s d) -> p s d", s=SUB),
                             rows[bass.ds(g, 1), :, :, :].rearrange("g p s d -> (g p) s d")).then_inc(s_small, 16)

            scan(0)
            with sp.Fori(0, NG - 1) as g:
                small(0, g)
                sp.wait_ge(s_small, 32 * g + 32)
                apart(sp)
                scan(g + 1)
            small(0, NG - 1)
            sp.wait_ge(s_small, 32 * NG)
            sp.wait_ge(s_st, 32 * NG)
            with sp.Fori(0, NG) as g:
                small(1, g)
                sp.wait_ge(s_small, 32 * NG + 16 * g + 16)
                apart(sp)
            sp.wait_ge(s_out, 16 * NG)

        @block.gpsimd
        def _(pool):
            nc.gpsimd.memset(ones[:, :], 1.0).then_inc(s_ones, 1)
            nc.gpsimd.memset(onesC[:, :], 1.0)
            nc.gpsimd.memset(zrow[:, :], 0.0)
            nc.gpsimd.memset(hrow[:, :, DEN:DEN + 1], 1.0)
            nc.gpsimd.iota(iota_q[:, :], [[1, P]], base=0, channel_multiplier=0, allow_small_or_imprecise_dtypes=True)
            nc.gpsimd.iota(iota_r[:, :], [[1, C]], base=-1024, channel_multiplier=0, allow_small_or_imprecise_dtypes=True)
            nc.gpsimd.iota(iota_slot[:, :], [[P, C]], base=0, channel_multiplier=1, allow_small_or_imprecise_dtypes=True)
            nc.gpsimd.iota(iota_turn[:, :], [[P * U, TURNS]], base=0, channel_multiplier=0,
                           allow_small_or_imprecise_dtypes=True)
            nc.gpsimd.iota(j_i[:, :], [[1, C]], base=0, channel_multiplier=C)
            pool.wait_ge(s_ones, 1)
            nc.gpsimd.affine_select(out=ident[:, :], in_=ones[:, :], pattern=[[1, P]], compare_op=ALU.is_equal,
                                    fill=0.0, base=0, channel_multiplier=-1)
            nc.gpsimd.affine_select(out=before[:, :], in_=ones[:, :], pattern=[[1, P]], compare_op=ALU.is_gt,
                                    fill=0.0, base=0, channel_multiplier=-1)
            nc.gpsimd.memset(group_first[:, :], 0.0).then_inc(s_const, 1)

            def gathers(layer, g):
                lo, hi = rounds(pool, layer, g)
                with pool.Fori(lo, hi) as k:
                    at = turn(pool, k, lo) * U + g * C
                    for u in range(U):
                        w = D if layer == 0 else HW
                        pool.wait_ge(s_v, k * U + u + 1)
                        if layer == 0:
                            pool.wait_ge(s_tr, k * U + u + 1)
                        pool.wait_ge(s_fill, k * U + u + 1)
                        apart(pool)
                        nc.gpsimd.tensor_copy(idx[:, u, :], lists[:, bass.ds(at + u, 1), :].rearrange("p o t -> p (o t)")
                                              ).then_inc(s_idx, 1)
                        pool.wait_ge(s_idx, k * U + u + 1)
                        apart(pool)
                        pool.indirect_dma_start(
                            out=st_feat[:, u, 0:w], out_offset=None, in_=(feat if layer == 0 else table),
                            in_offset=bass.IndirectOffsetOnAxis(idx[:, u, 0:1].bitcast(U32), 0),
                            ).then_inc(s_gf[u], 16)
                        pool.indirect_dma_start(
                            out=st_mask[:, u, :], out_offset=None, in_=mask_rows,
                            in_offset=bass.IndirectOffsetOnAxis(idx[:, u, 1:2].bitcast(U32), 0),
                            ).then_inc(s_gm[u], 16)

            with pool.Fori(0, NG) as g:
                pool.wait_ge(s_list, g + 1)
                gathers(0, g)
            pool.wait_ge(s_bounds1, 1)
            pool.wait_ge(s_st, 32 * NG)
            with pool.Fori(0, NG) as g:
                gathers(1, g)

        @block.scalar
        def _(act):
            act.sem_inc(s_v, U)
            act.sem_inc(s_kt, 1)
            act.sem_inc(s_fill, U)
            act.sem_inc(s_piece_a, RING)
            act.wait_ge(s_wx, 1)
            nc.scalar.copy(w1x[:, COLT:COLT + 1], ps_X[:, 1:2])
            nc.scalar.copy(w1x[:, ROWT:ROWT + 1], ps_X[:, 0:1]).then_inc(s_w1x, 1)
            act.wait_ge(s_mean, 1)
            nc.scalar.mul(mean0[:, :], ps_X[:, 0:D], 1.0 / N).then_inc(s_meanc, 1)

            def scan(g):
                act.wait_ge(s_occ_free, g + 1)
                for n in range(PIECES):
                    act.wait_ge(s_scan[n % RING], (g * PER_RING + n // RING) * 16 + 16)
                    for c in range(PC - ACT_COLS, PC):
                        last = nc.scalar.activation(scan_buf[:, n % RING, c, :], scan_buf[:, n % RING, c, :], ACT.Relu,
                                                    accum_out=occ[:, n * PC + c:n * PC + c + 1])
                    last.then_inc(s_piece_a, 1)

            def attend(layer, g):
                gg = g + layer * NG
                lo, hi = rounds(act, layer, g)
                act.wait_ge(s_pre, gg + 1)
                if layer == 0:
                    nc.scalar.copy(qT[:, :], ps_B[:, :]).then_inc(s_q, 1)
                act.wait_ge(s_O, gg + 1)
                with act.Fori(lo, hi) as k:
                    r = turn(act, k, lo) * U
                    for u in range(U):
                        act.wait_ge(s_gf[u], 16 * k + 16)
                        w = D if layer == 0 else HW
                        nc.scalar.copy(V[:, bass.ds((r + u) * HW, w)], st_feat[:, u, 0:w]).then_inc(s_v, 1)
                    if layer == 0:
                        act.wait_ge(s_tr, k * U + 2 * U)
                        act.wait_ge(s_sub, k * U + U)
                        nc.scalar.copy(kT[:, :, :], ps_T[:, :, :]).then_inc(s_kt, 1)
                    for u in range(U):
                        act.wait_ge(s_gm[u], 16 * k + 16)
                        act.wait_ge(s_sub, k * U + u + 1)
                        if layer == 1:
                            nc.scalar.activation(stage[:, u, :], ps_B[:, :], ACT.Identity,
                                                 bias=st_feat[:, u, COLT:COLT + 1]).then_inc(s_raw, 1)
                        nc.scalar.activation(fill[:, u, :], st_mask[:, u, :], ACT.Relu, scale=-BIG,
                                             bias=pad_bias[:, bass.ds(g * C + r + u, 1)]).then_inc(s_fill, 1)
                with act.Fori(lo, hi) as k:
                    r = turn(act, k, lo) * U
                    for u in range(U):
                        act.wait_ge(s_dif, k * U + u + 1)
                        act.wait_ge(s_pv, k * U + u + 1)
                        nc.scalar.activation(stage[:, u, :], S[:, bass.ds((r + u) * G, G)], ACT.Exp,
                                             scale=(1.0 / TEMPERATURE if layer == 0 else 1.0)).then_inc(s_p, 1)
                if layer == 0:
                    act.wait_ge(s_xT, g + 1)
                    nc.scalar.activation(xnT[:, :], ps_X[:, 0:G], ACT.Copy,
                                         accum_out=xsum[:, bass.ds(g, 1)]).then_inc(s_xTc, 1)
                    act.wait_ge(s_h, g + 1)
                    act.wait_ge(s_st, 32 * g)
                    hx = ps_X[:, 0:SUB * WX].rearrange("p (s w) -> p s w", s=SUB)
                    nc.scalar.copy(hrow[:, :, 0:D], hx[:, :, 0:D])
                    nc.scalar.copy(hrow[:, :, COLT:COLT + 1], hx[:, :, COLT:COLT + 1]).then_inc(s_hc, 1)
                    act.wait_ge(s_hc, g + 1)
                    act.dma_start(table_rows[bass.ds(g, 1), :, :, :].rearrange("g p s d -> (g p) s d"),
                                  hrow[:, :, :]).then_inc(s_st, 16)
                    act.wait_ge(s_xn, gg + 1)
                    act.dma_start(x1_rows[bass.ds(g, 1), :, :, :].rearrange("g p s d -> (g p) s d"),
                                  xn[:, :, :]).then_inc(s_st, 16)
                else:
                    act.wait_ge(s_xn, gg + 1)
                    act.dma_start(out_rows[bass.ds(g, 1), :, :, :].rearrange("g p s d -> (g p) s d"),
                                  xn[:, :, :]).then_inc(s_out, 16)

            scan(0)
            with act.Fori(0, NG - 1) as g:
                scan(g + 1)
                attend(0, g)
            act.wait_ge(s_list, NG)
            attend(0, NG - 1)
            act.wait_ge(s_mean, 2)
            nc.scalar.copy(mean1[:, :], ps_X[:, 0:D]).then_inc(s_meanc, 1)
            act.wait_ge(s_bounds1, 1)
            with act.Fori(0, NG) as g:
                attend(1, g)
            act.wait_ge(s_out, 16 * NG)

        @block.tensor
        def _(pe):
            pe.sem_inc(s_tr, U)
            pe.sem_inc(s_O, 1)
            pe.sem_inc(s_pv, U)
            pe.wait_ge(s_const, 1)
            pe.wait_ge(s_load, 64)
            nc.tensor.matmul(ps_X[:, 0:2], w1T_sb[:, :], a_sb[:, :], start=True, stop=True).then_inc(s_wx, 1)
            pe.wait_ge(s_w1x, 1)
            pe.wait_ge(s_feat, 16)
            for c in range(C):
                last = nc.tensor.matmul(ps_X[:, 0:D], ones[:, :], feat_all[:, c * D:(c + 1) * D],
                                        start=(c == 0), stop=(c == C - 1))
            last.then_inc(s_mean, 1)

            def compact(g):
                pe.wait_ge(s_tot, g + 1)
                nc.tensor.matmul(ps_L[:, 0:1], before[:, :], prefix[:, C - 1:C], start=True, stop=True)
                nc.tensor.matmul(ps_L[:, 1:2], ones[:, :], prefix[:, C - 1:C], start=True, stop=True
                                 ).then_inc(s_off, 1)
                parts = PIECES // 2
                for n in range(parts):
                    pe.wait_ge(s_hot, g * parts + n + 1)
                    for c in range(C // parts):
                        cc = n * (C // parts) + c
                        last = nc.tensor.matmul(ps_L[:, 128:128 + 2 * C], onehot_q[:, hot_buf(n), c, :],
                                                j_rounds[:, cc, :, :].rearrange("p k r -> p (k r)"),
                                                start=(cc == 0), stop=(cc == C - 1))
                    last.then_inc(s_hot_free if n < parts - 1 else s_listp, 1)

            def attend(layer, g):
                gg = g + layer * NG
                lo, hi = rounds(pe, layer, g)
                pe.wait_ge(s_O_free, gg + 1)
                if layer == 0:
                    pe.wait_ge(s_small, 32 * g + 32)
                    nc.tensor.matmul(ps_B[:, :], w0_sb[:, :], xT_sb[:, bass.ds((g % 2) * G, G)],
                                     start=True, stop=True).then_inc(s_pre, 1)
                    pe.wait_ge(s_q, g + 1)
                    apart(pe)
                else:
                    pe.wait_ge(s_diag, NG + 2 * g + 1)
                    nc.tensor.matmul(ps_B[:, :], ones[:, :], diag[:, :, :].rearrange("p s i -> p (s i)"),
                                     start=True, stop=True).then_inc(s_pre, 1)
                if layer == 0:
                    with pe.Fori(lo, hi) as k:
                        pe.wait_ge(s_kt, k + 1)
                        for u in range(U):
                            pe.wait_ge(s_gf[u], 16 * k + 16)
                            nc.tensor.transpose(ps_T[:, u, :], st_feat[:, u, 0:D], ident[:, :]).then_inc(s_tr, 1)
                        for u in range(U):
                            pe.wait_ge(s_kt, k + 2)
                            pe.wait_ge(s_sub, k * U + u + 1)
                            nc.tensor.matmul(ps_S[u][:, :], kT[:, u, :], qT[:, :], start=True, stop=True
                                             ).then_inc(s_raw, 1)
                pe.wait_ge(s_max, gg + 1)
                for s in range(SUB):
                    last = nc.tensor.transpose(ps_B[:, s * P:(s + 1) * P], M[:, s * P:(s + 1) * P], ident[:, :])
                last.then_inc(s_mT, 1)
                pe.wait_ge(s_diag, gg + 1 if layer == 0 else NG + 2 * g + 2)
                nc.tensor.matmul(ps_B[:, :], ones[:, :], diag[:, :, :].rearrange("p s i -> p (s i)"),
                                 start=True, stop=True).then_inc(s_mb, 1)
                nc.tensor.matmul(ps_O[:, :, :].rearrange("p s d -> p (s d)"), zrow[:, 0:P], zrow[:, 0:SUB * (D + 1)],
                                 start=True, stop=False, skip_group_check=True)
                with pe.Fori(lo, hi) as k:
                    r = turn(pe, k, lo) * U
                    for u in range(U):
                        pe.wait_ge(s_p, k * U + u + 1)
                        for s in range(SUB):
                            last = nc.tensor.matmul(ps_O[:, s, :], stage[:, u, s * P:(s + 1) * P],
                                                    V[:, bass.ds((r + u) * HW, D + 1)], start=False, stop=False,
                                                    skip_group_check=True)
                        last.then_inc(s_pv, 1)
                nc.tensor.matmul(ps_O[:, :, :].rearrange("p s d -> p (s d)"), zrow[:, 0:P], zrow[:, 0:SUB * (D + 1)],
                                 start=False, stop=True, skip_group_check=True).then_inc(s_O, 1)
                if layer == 0:
                    pe.wait_ge(s_xn, gg + 1)
                    for s in range(SUB):
                        last = nc.tensor.transpose(ps_X[:, s * P:(s + 1) * P], xn[:, s, :], ident[:, :])
                    last.then_inc(s_xT, 1)
                    pe.wait_ge(s_xTc, g + 1)
                    for s in range(SUB):
                        last = nc.tensor.matmul(ps_X[:, s * WX:(s + 1) * WX], xnT[:, s * P:(s + 1) * P], w1x[:, :],
                                                start=(s == 0), stop=True, skip_group_check=True)
                    last.then_inc(s_h, 1)

            pe.wait_ge(s_vconst, 1)
            pe.wait_ge(s_meanc, 1)
            compact(0)
            with pe.Fori(0, NG - 1) as g:
                compact(g + 1)
                attend(0, g)
            attend(0, NG - 1)
            pe.wait_ge(s_xmean, 1)
            nc.tensor.matmul(ps_X[:, 0:D], xmean_b[:, :], w1x[:, 0:D], start=True, stop=True).then_inc(s_mean, 1)
            pe.wait_ge(s_bounds1, 1)
            with pe.Fori(0, NG) as g:
                attend(1, g)

        @block.vector
        def _(dve):
            dve.sem_inc(s_sub, U)
            dve.sem_inc(s_piece_v, RING)
            dve.sem_inc(s_occ_free, 1)
            dve.sem_inc(s_small_free, 2)
            dve.sem_inc(s_O_free, 1)
            nc.vector.memset(V[:, :].rearrange("p (r w) -> p r w", w=HW)[:, :, DEN:DEN + 1], 1.0)
            nc.vector.memset(turn_sum[:, :], 0.0)
            nc.vector.memset(bounds[:, :], 0)
            nc.vector.memset(w1x[:, DEN:DEN + 1], 0.0)
            dve.wait_ge(s_const, 1)
            nc.vector.tensor_scalar(pos[:, :], j_i[:, :], 6, None, ALU.arith_shift_right)
            nc.vector.tensor_scalar(pos_low[:, :], j_i[:, :], JSPLIT - 1, None, ALU.bitwise_and)
            dve.drain()
            nc.vector.tensor_copy(j_high[:, :], pos[:, :])
            nc.vector.tensor_copy(j_low[:, :], pos_low[:, :])
            dve.drain()
            nc.vector.memset(M[:, :], LEAST).then_inc(s_vconst, 1)

            def scan(g):
                V_COLS = PC - ACT_COLS
                for n in range(PIECES):
                    dve.wait_ge(s_scan[n % RING], (g * PER_RING + n // RING) * 16 + 16)
                    nc.vector.tensor_reduce(occ[:, n * PC:n * PC + V_COLS], scan_buf[:, n % RING, 0:V_COLS, :],
                                            AX.X, ALU.max).then_inc(s_piece_v, 1)
                dve.drain()
                dve.wait_ge(s_piece_a, g * PIECES + PIECES + RING)
                nc.vector.tensor_scalar(present[:, :], occ[:, :], 0.0, None, ALU.is_gt).then_inc(s_occ_free, 1)
                dve.drain()
                nc.vector.tensor_tensor_scan(prefix[:, :], onesC[:, :], present[:, :], 0.0, ALU.mult, ALU.add
                                             ).then_inc(s_tot, 1)
                dve.wait_ge(s_off, g + 1)
                nc.vector.tensor_copy(offs[:, :], ps_L[:, 0:2])
                dve.drain()
                nc.vector.scalar_tensor_tensor(out=pos[:, :], in0=prefix[:, :], scalar=offs[:, 0:1],
                                               in1=present[:, :], op0=ALU.add, op1=ALU.subtract)
                dve.drain()
                nc.vector.tensor_scalar(pos_low[:, :], pos[:, :], P - 1, None, ALU.bitwise_and)
                nc.vector.tensor_scalar(pos_high[:, :], pos[:, :], 7, None, ALU.arith_shift_right)
                dve.drain()
                nc.vector.scalar_tensor_tensor(out=pos_round[:, :], in0=present[:, :], scalar=-1024.0,
                                               in1=pos_high[:, :], op0=ALU.mult, op1=ALU.add)
                dve.drain()
                nc.vector.tensor_tensor(onehot_r[:, :, :], pos_round[:, :].unsqueeze(2).to_broadcast([P, C, C]),
                                        iota_r[:, :].unsqueeze(1).to_broadcast([P, C, C]), ALU.is_equal)
                dve.drain()
                nc.vector.tensor_tensor(j_rounds[:, :, 0, :], onehot_r[:, :, :],
                                        j_high[:, :].unsqueeze(2).to_broadcast([P, C, C]), ALU.mult)
                nc.vector.tensor_tensor(j_rounds[:, :, 1, :], onehot_r[:, :, :],
                                        j_low[:, :].unsqueeze(2).to_broadcast([P, C, C]), ALU.mult)
                parts = PIECES // 2
                CP = C // parts
                for n in range(parts):
                    if n == 2:
                        dve.wait_ge(s_hot_free, g * (parts - 1) + 1)
                    nc.vector.tensor_tensor(
                        onehot_q[:, hot_buf(n), :, :],
                        pos_low[:, n * CP:(n + 1) * CP].unsqueeze(2).to_broadcast([P, CP, P]),
                        iota_q[:, :].unsqueeze(1).to_broadcast([P, CP, P]), ALU.is_equal).then_inc(s_hot, 1)
                nc.vector.tensor_scalar(pad_tmp[:, :], iota_slot[:, :], offs[:, 1:2], HUGE, ALU.is_ge, ALU.mult)
                nc.vector.tensor_scalar(turn_flags[:, :], iota_turn[:, :], offs[0:1, 1:2], None, ALU.is_lt)
                dve.drain()
                nc.vector.tensor_scalar(pad_bias[:, bass.ds(g * C, C)], pad_tmp[:, :], BIG, None, ALU.add)
                nc.vector.tensor_reduce(turn_n[:, :], turn_flags[:, :], AX.X, ALU.add)
                dve.drain()
                nc.vector.scalar_tensor_tensor(out=turn_sum[:, :], in0=turn_n[:, :], scalar=1.0,
                                               in1=turn_sum[:, :], op0=ALU.max, op1=ALU.add)
                dve.drain()
                nc.vector.tensor_copy(bounds[0:1, bass.ds(g + 1, 1)], turn_sum[:, :])
                dve.wait_ge(s_listp, g + 1)
                nc.vector.tensor_scalar(list_high[:, :], ps_L[:, 128:128 + C], float(JSPLIT), None, ALU.mult)
                dve.drain()
                nc.vector.tensor_tensor(lists[:, bass.ds(g * C, C), 0], ps_L[:, 128 + C:128 + 2 * C], list_high[:, :],
                                        ALU.add)
                nc.vector.scalar_tensor_tensor(out=lists[:, bass.ds(g * C, C), 1],
                                               in0=ps_L[:, 128 + C:128 + 2 * C], scalar=group_first[:, 0:1],
                                               in1=list_high[:, :], op0=ALU.add, op1=ALU.add)
                dve.drain()
                nc.vector.tensor_scalar(group_first[:, :], group_first[:, :], float(N), None, ALU.add
                                        ).then_inc(s_list, 1)

            def attend(layer, g):
                gg = g + layer * NG
                lo, hi = rounds(dve, layer, g)
                if layer == 1:
                    nc.vector.tensor_tensor(diag[:, :, :], ident[:, :].unsqueeze(1).to_broadcast([P, SUB, P]),
                                            s1col[:, bass.ds(g * SUB, SUB)].unsqueeze(2).to_broadcast([P, SUB, P]),
                                            ALU.mult).then_inc(s_diag, 1)
                dve.wait_ge(s_O, gg + 1)
                apart(dve)
                with dve.Fori(lo, hi) as k:
                    r = turn(dve, k, lo) * U
                    if layer == 1:
                        for u in range(U):
                            dve.wait_ge(s_raw, k * U + u + 1)
                            nc.vector.scalar_tensor_tensor(out=stage[:, u, :], in0=stage[:, u, :], scalar=SLOPE,
                                                           in1=stage[:, u, :], op0=ALU.mult, op1=ALU.max)
                        dve.drain()
                    for u in range(U):
                        if layer == 0:
                            dve.wait_ge(s_raw, k * U + u + 1)
                        dve.wait_ge(s_fill, k * U + u + 1 + U)
                        raw = ps_S[u][:, :] if layer == 0 else stage[:, u, :]
                        nc.vector.tensor_tensor(S[:, bass.ds((r + u) * G, G)], raw, fill[:, u, :], ALU.subtract
                                                ).then_inc(s_sub, 1)
                    for u in range(U):
                        dve.drain()
                        nc.vector.tensor_tensor(M[:, :], M[:, :], S[:, bass.ds((r + u) * G, G)], ALU.max)
                dve.drain()
                nc.vector.tensor_copy(mcol[:, 0:1], M[:, 0:1]).then_inc(s_max, 1)
                dve.wait_ge(s_mT, gg + 1)
                nc.vector.tensor_reduce(mcol[:, :], ps_B[:, :].rearrange("p (s q) -> p s q", s=SUB), AX.X, ALU.max)
                nc.vector.memset(M[:, :], LEAST)
                dve.drain()
                nc.vector.tensor_tensor(diag[:, :, :], ident[:, :].unsqueeze(1).to_broadcast([P, SUB, P]),
                                        mcol[:, :].unsqueeze(2).to_broadcast([P, SUB, P]), ALU.mult
                                        ).then_inc(s_diag, 1)
                dve.wait_ge(s_mb, gg + 1)
                apart(dve)
                with dve.Fori(lo, hi) as k:
                    r = turn(dve, k, lo) * U
                    for u in range(U):
                        nc.vector.tensor_tensor(S[:, bass.ds((r + u) * G, G)], S[:, bass.ds((r + u) * G, G)],
                                                ps_B[:, :], ALU.subtract).then_inc(s_dif, 1)
                nc.vector.tensor_scalar(empty[:, :], mcol[:, :], -BIG / 2, None, ALU.is_lt)
                nc.vector.tensor_scalar(full[:, :], mcol[:, :], -BIG / 2, None, ALU.is_ge)
                dve.wait_ge(s_O, gg + 2)
                nc.vector.reciprocal(rden[:, :], ps_O[:, :, DEN:DEN + 1].rearrange("p s o -> p (s o)"))
                dve.drain()
                nc.vector.tensor_tensor(rdf[:, :], rden[:, :], full[:, :], ALU.mult)
                dve.drain()
                if layer == 0:
                    dve.wait_ge(s_small, 32 * g + 32)
                else:
                    dve.wait_ge(s_small, 32 * NG + 16 * g + 16)
                    dve.wait_ge(s_meanc, 2)
                for s in range(SUB):
                    last = nc.vector.scalar_tensor_tensor(out=y[:, s, :], in0=ps_O[:, s, 0:D], scalar=rdf[:, s:s + 1],
                                                          in1=xres[:, bass.ds((g % 2) * G + s * D, D)],
                                                          op0=ALU.mult, op1=ALU.add)
                last.then_inc(s_small_free, 1)
                dve.drain()
                for s in range(SUB):
                    last = nc.vector.scalar_tensor_tensor(out=y[:, s, :], in0=(mean0 if layer == 0 else mean1)[:, :],
                                                          scalar=empty[:, s:s + 1], in1=y[:, s, :],
                                                          op0=ALU.mult, op1=ALU.add)
                last.then_inc(s_O_free, 1)
                dve.drain()
                for s in range(SUB):
                    nc.vector.bn_stats(stats[:, s, :], y[:, s, :])
                dve.drain()
                for s in range(SUB):
                    nc.vector.bn_aggr(mv[:, s, :], stats[:, s, :])
                dve.drain()
                nc.vector.tensor_scalar(var[:, :], mv[:, :, 1:2].rearrange("p s o -> p (s o)"), EPS, None, ALU.add)
                dve.drain()
                nc.vector.tensor_scalar(half[:, :], var[:, :].bitcast(I32), 1, None, ALU.logical_shift_right)
                dve.drain()
                nc.vector.tensor_scalar(rstd[:, :].bitcast(I32), half[:, :], -1.0, float(0x5F3759DF),
                                        ALU.mult, ALU.add)
                for _ in range(3):
                    dve.drain()
                    nc.vector.tensor_tensor(rsq[:, :], rstd[:, :], rstd[:, :], ALU.mult)
                    dve.drain()
                    nc.vector.scalar_tensor_tensor(out=rsq[:, :], in0=rsq[:, :], scalar=-0.5, in1=var[:, :],
                                                   op0=ALU.mult, op1=ALU.mult)
                    dve.drain()
                    nc.vector.scalar_tensor_tensor(out=rstd[:, :], in0=rsq[:, :], scalar=1.5, in1=rstd[:, :],
                                                   op0=ALU.add, op1=ALU.mult)
                dve.drain()
                if layer == 0:
                    dve.wait_ge(s_st, 32 * g)
                else:
                    dve.wait_ge(s_st, 32 * NG)
                    dve.wait_ge(s_out, 16 * g)
                for s in range(SUB):
                    last = nc.vector.tensor_scalar(xn[:, s, :], y[:, s, :], mv[:, s, 0:1], rstd[:, s:s + 1],
                                                   ALU.subtract, ALU.mult)
                last.then_inc(s_xn, 1)
                if layer == 0:
                    dve.wait_ge(s_h, g + 1)
                    dve.wait_ge(s_hc, g + 1)
                    nc.vector.tensor_copy(s1col[:, bass.ds(g * SUB, SUB)],
                                          ps_X[:, 0:SUB * WX].rearrange("p (s w) -> p s w", s=SUB)[:, :, ROWT:WX]
                                          .rearrange("p s o -> p (s o)")).then_inc(s_s1, 1)

            scan(0)
            with dve.Fori(0, NG - 1) as g:
                scan(g + 1)
                attend(0, g)
            nc.vector.tensor_scalar(bounds[0:1, NG + 1:2 * NG + 2], bounds[0:1, 0:NG + 1], turn_sum[0:1, 0:1], None,
                                    ALU.add).then_inc(s_bounds1, 1)
            attend(0, NG - 1)
            dve.wait_ge(s_xTc, NG)
            nc.vector.tensor_reduce(xmean[:, :], xsum[:, :], AX.X, ALU.add)
            dve.drain()
            nc.vector.tensor_scalar(xmean_b[:, :], ones[:, :], xmean[:, 0:1], 1.0 / N, ALU.mult, ALU.mult
                                    ).then_inc(s_xmean, 1)
            dve.wait_ge(s_bounds1, 1)
            with dve.Fori(0, NG) as g:
                attend(1, g)


def hot_buf(n):
    return n % 2


def kernel(**inputs):
    import numpy as np
    import concourse.bacc as bacc
    from concourse import mybir as mb
    from concourse.bass_utils import run_bass_kernel_spmd

    x = np.ascontiguousarray(inputs["x"])
    adj = np.asarray(inputs["adj"])
    n, d = x.shape
    arrays = {
        "x": x,
        "xT": np.ascontiguousarray(x.T),
        "adjT": np.ascontiguousarray(adj.reshape(n // G, G, n).transpose(0, 2, 1)),
        "feat": np.ascontiguousarray(inputs["L0_gnn_input"]),
        "w0": np.ascontiguousarray(inputs["L0_gnn_weight"]),
        "w1": np.ascontiguousarray(inputs["L1_gnn_W"]),
        "w1T": np.ascontiguousarray(np.asarray(inputs["L1_gnn_W"]).T),
        "a": np.ascontiguousarray(np.asarray(inputs["L1_gnn_a"]).reshape(2, d).T),
    }
    nc = bacc.Bacc("TRN2", target_bir_lowering=False, num_devices=1)
    args = [nc.dram_tensor(f"in_{k}", v.shape, mb.dt.from_np(v.dtype), kind="ExternalInput").ap()
            for k, v in arrays.items()]
    x1_dram = nc.dram_tensor("x1_dram", (n, d), F32, kind="Internal").ap()
    table = nc.dram_tensor("table", (n, d + 2), F32, kind="Internal").ap()
    out = nc.dram_tensor("out_x", (n, d), F32, kind="ExternalOutput").ap()
    graph_attention_kernel(nc, *args, x1_dram, table, out)
    r = run_bass_kernel_spmd(nc, [{f"in_{k}": v for k, v in arrays.items()}], core_ids=[0])
    return r.results[0]["out_x"]
```

```python
from contextlib import ExitStack

import concourse.bass as bass
from concourse import mybir

P = 128
U = 3
SUB = 3
G = SUB * P
PIECES = 12
RING = 4
STAGES = ((0, 2), (2, 8), (8, 12))
ACT_COLS = 1
TEMPERATURE = 0.07
SLOPE = 0.01
EPS = 1e-5
BIG = 2.0 ** 60
LEAST = -3.0e38

ALU = mybir.AluOpType
ACT = mybir.ActivationFunctionType
AX = mybir.AxisListType
F32 = mybir.dt.float32
BF16 = mybir.dt.bfloat16
I32 = mybir.dt.int32
U32 = mybir.dt.uint32


def graph_attention_kernel(nc, x, xT, adjT, feat, w0, w1, w1T, a, x1_dram, table, masks, out):
    N, D = feat.shape
    NG = N // G
    C = N // P
    PC = C // PIECES
    PER_RING = PIECES // RING
    V_COLS = PC - ACT_COLS
    TURNS = C // U
    DEN = D
    COLT, COLTS = D + 1, D + 2
    HW = D + 3
    ROWT = D + 3
    WX = D + 4
    PADROW = NG * N
    LOC = C + 2

    scan_src = adjT[0:NG * N, :].rearrange("(g p c) i -> g p c i", c=C, p=P)
    x_rows = x.rearrange("(g s p) d -> g p s d", s=SUB, p=P)
    x1_rows = x1_dram.rearrange("(g s p) d -> g p s d", s=SUB, p=P)
    out_rows = out.rearrange("(g s p) d -> g p s d", s=SUB, p=P)
    table_rows = table.rearrange("(g s p) d -> g p s d", s=SUB, p=P)
    xT_groups = xT.rearrange("d (g i) -> g d i", i=G)

    with ExitStack() as ctx:
        def sb(name, shape, dt=F32):
            return ctx.enter_context(nc.sbuf_tensor(name, shape, dt))

        def pb(name, shape, dt=F32):
            return ctx.enter_context(nc.psum_tensor(name, shape, dt))

        def sem(name):
            return ctx.enter_context(nc.semaphore(name))

        ident = sb("ident", [P, P])
        before = sb("before", [P, P])
        shift = sb("shift", [P, P])
        steps = sb("steps", [P, P])
        ones = sb("ones", [P, P])
        mask_w = sb("mask_w", [P, P], BF16)
        zrow = sb("zrow", [1, 512], BF16)
        big = sb("big", [P, 1])
        iota_s = sb("iota_s", [P, U * P])
        iota_turn = sb("iota_turn", [1, TURNS])
        onesC = sb("onesC", [P, C])
        w0_sb = sb("w0_sb", [P, D])
        w1x = sb("w1x", [P, WX])
        w1T_sb = sb("w1T_sb", [P, D])
        a_sb = sb("a_sb", [P, 2])
        mean0 = sb("mean0", [P, D])
        mean1 = sb("mean1", [P, D])
        scan_buf = sb("scan_buf", [P, RING, PC, G], I32)
        occ = sb("occ", [P, C])
        present = sb("present", [P, C])
        prefix = sb("prefix", [P, C])
        local = sb("local", [P, LOC], BF16)
        offs = sb("offs", [P, 2])
        first = sb("first", [P, 1])
        reached = sb("reached", [P, U * P], BF16)
        place_i = sb("place_i", [P, U], I32)
        place0 = sb("place0", [P, U])
        place = sb("place", [P, U])
        real = sb("real", [P, U])
        rank = sb("rank", [P, U])
        ahead = sb("ahead", [P, U, C])
        ccol = sb("ccol", [P, U])
        jcol = sb("jcol", [P, U])
        mrow = sb("mrow", [P, U])
        group_row = sb("group_row", [P, 1])
        lists = sb("lists", [P, NG * C, 2], I32)
        turn_flags = sb("turn_flags", [1, TURNS])
        turn_n = sb("turn_n", [1, 1])
        turn_sum = sb("turn_sum", [1, 1])
        bounds = sb("bounds", [1, 2 * (NG + 1)], I32)
        idx = sb("idx", [P, U, 2], I32)
        st_feat = sb("st_feat", [P, U, HW])
        st_mask = sb("st_mask", [P, U, G], I32)
        V = sb("V", [P, C * HW])
        F = sb("F", [P, C * G], BF16)
        S = sb("S", [P, C * G])
        kst = sb("kst", [P, U, P])
        kT = sb("kT", [P, U, P])
        fill = sb("fill", [P, U, G], BF16)
        prob = sb("prob", [P, U, G])
        M = sb("M", [P, G])
        mcol = sb("mcol", [P, SUB])
        mrow_t = sb("mrow_t", [P, SUB])
        rterm = sb("rterm", [P, 2, SUB])
        diag = sb("diag", [P, SUB, P])
        xT_sb = sb("xT_sb", [P, 2 * G])
        xres = sb("xres", [P, 2 * G])
        qT = sb("qT", [P, G])
        rden = sb("rden", [P, SUB])
        full = sb("full", [P, SUB])
        rdf = sb("rdf", [P, SUB])
        empty = sb("empty", [P, SUB])
        y = sb("y", [P, SUB, D])
        stats = sb("stats", [P, SUB, 6])
        mv = sb("mv", [P, SUB, 2])
        mvs = sb("mvs", [P, NG * SUB, 2])
        rstd = sb("rstd", [P, NG * SUB])
        var = sb("var", [P, NG * SUB])
        half = sb("half", [P, NG * SUB], I32)
        rsq = sb("rsq", [P, NG * SUB])
        xn = sb("xn", [P, SUB, D])
        xsum = sb("xsum", [P, NG])
        xmean = sb("xmean", [P, 1])
        hrow = sb("hrow", [P, SUB, HW])
        s1col = sb("s1col", [P, NG * SUB])

        ps_T = pb("ps_T", [P, U, P])
        ps_S = pb("ps_S", [P, U, 512])
        ps_O = pb("ps_O", [P, SUB, D + 1])
        ps_B = pb("ps_B", [P, G])
        ps_L = pb("ps_L", [P, 512])
        ps_X = pb("ps_X", [P, 512])

        s_load = sem("s_load")
        s_feat = sem("s_feat")
        s_ones = sem("s_ones")
        s_const = sem("s_const")
        s_vconst = sem("s_vconst")
        s_wx = sem("s_wx")
        s_w1x = sem("s_w1x")
        s_mean = sem("s_mean")
        s_meanc = sem("s_meanc")
        s_xmean = sem("s_xmean")
        s_scan = [sem(f"s_scan{b}") for b in range(RING)]
        s_piece_v = sem("s_piece_v")
        s_piece_a = sem("s_piece_a")
        s_occ_free = sem("s_occ_free")
        s_tot = sem("s_tot")
        s_off = sem("s_off")
        s_bound = sem("s_bound")
        s_reach = sem("s_reach")
        s_pick = sem("s_pick")
        s_list = sem("s_list")
        s_small = sem("s_small")
        s_small_free = sem("s_small_free")
        s_apart = sem("s_apart")
        s_idx = sem("s_idx")
        s_gf = [sem(f"s_gf{u}") for u in range(U)]
        s_gm = [sem(f"s_gm{u}") for u in range(U)]
        s_feed = sem("s_feed")
        s_kst = sem("s_kst")
        s_tr = sem("s_tr")
        s_kt = sem("s_kt")
        s_fill = sem("s_fill")
        s_mst = sem("s_mst")
        s_raw = sem("s_raw")
        s_sc = sem("s_sc")
        s_max = sem("s_max")
        s_mT = sem("s_mT")
        s_diag = sem("s_diag")
        s_mb = sem("s_mb")
        s_dif = sem("s_dif")
        s_p = sem("s_p")
        s_pv = sem("s_pv")
        s_pre = sem("s_pre")
        s_q = sem("s_q")
        s_O = sem("s_O")
        s_O_free = sem("s_O_free")
        s_xn = sem("s_xn")
        s_xT = sem("s_xT")
        s_xTc = sem("s_xTc")
        s_h = sem("s_h")
        s_hc = sem("s_hc")
        s_st = sem("s_st")
        s_out = sem("s_out")

        feat_all = S[:, 0:C * D]
        xnT = qT
        diag_flat = xn
        y_all = scan_buf[:, :, :, :].rearrange("p b c i -> p (b c i)")[:, 0:NG * G].bitcast(F32)
        block = ctx.enter_context(nc.Block())

        def rounds(eng, layer, g):
            at = layer * (NG + 1)
            lo = eng.value_load(bounds[0:1, bass.ds(g + at, 1)], min_val=0, max_val=2 * NG * TURNS)
            hi = eng.value_load(bounds[0:1, bass.ds(g + at + 1, 1)], min_val=1, max_val=2 * NG * TURNS)
            return lo, hi

        def ring(eng, k):
            return eng.snap((k % TURNS) * U)

        def listed(eng, k, before_layer):
            at = k if before_layer is None else nc.s_assert_within(
                k - before_layer, 0, NG * TURNS - 1, skip_runtime_bounds_check_because="layer 1 repeats layer 0's turns")
            return eng.snap(nc.s_assert_within(
                at, 0, NG * TURNS - 1, skip_runtime_bounds_check_because="a group has at most TURNS turns"))

        def apart(eng):
            eng.sem_inc(s_apart, 1)

        @block.sync
        def _(sp):
            sp.dma_start(w0_sb[:, :], w0).then_inc(s_load, 16)
            sp.dma_start(w1x[:, 0:D], w1).then_inc(s_load, 16)
            sp.dma_start(w1T_sb[:, :], w1T).then_inc(s_load, 16)
            sp.dma_start(a_sb[:, :], a).then_inc(s_load, 16)
            sp.dma_start(feat_all, feat.rearrange("(p c) d -> p (c d)", c=C)).then_inc(s_feat, 16)

            def scan(g):
                for n in range(PIECES):
                    sp.wait_ge(s_piece_v, g * PIECES + n + 1)
                    sp.wait_ge(s_piece_a, g * PIECES + n + 1)
                    sp.dma_start(scan_buf[:, n % RING, :, :],
                                 scan_src[bass.ds(g, 1), :, n * PC:(n + 1) * PC, :].rearrange("g p c i -> (g p) c i")
                                 ).then_inc(s_scan[n % RING], 16)

            def small(layer, g):
                if layer == 1:
                    sp.wait_ge(s_small, 32 * NG + 16 * g)
                elif not isinstance(g, int) or g > 0:
                    sp.wait_ge(s_small, 32 * g)
                apart(sp)
                sp.wait_ge(s_small_free, g + layer * NG + 1)
                apart(sp)
                at = bass.ds((g % 2) * G, G)
                if layer == 0:
                    sp.dma_start(xT_sb[:, at], xT_groups[bass.ds(g, 1), :, :].rearrange("g d i -> (g d) i")
                                 ).then_inc(s_small, 16)
                rows = x_rows if layer == 0 else x1_rows
                sp.dma_start(xres[:, at].rearrange("p (s d) -> p s d", s=SUB),
                             rows[bass.ds(g, 1), :, :, :].rearrange("g p s d -> (g p) s d")).then_inc(s_small, 16)

            scan(0)
            small(0, 0)
            scan(1)
            with sp.Fori(0, NG - 2) as g:
                small(0, sp.snap(g + 1))
                scan(sp.snap(g + 2))
            small(0, NG - 1)
            sp.wait_ge(s_st, 32 * NG + 32)
            total = sp.value_load(bounds[0:1, NG:NG + 1], min_val=1, max_val=NG * TURNS)
            with sp.Fori(0, NG) as g:
                lo, hi = rounds(sp, 1, g)
                with sp.Fori(lo, hi) as k:
                    sp.wait_ge(s_pv, k * U + U)
                    sp.wait_ge(s_mst, k * 16 + 16)
                    apart(sp)
                    sp.dma_start(F[:, bass.ds(ring(sp, k) * G, U * G)].rearrange("p (u i) -> p u i", u=U),
                                 masks[bass.ds(listed(sp, k, total), 1), :, :, :].rearrange("t p u i -> (t p) u i")
                                 ).then_inc(s_mst, 16)
                small(1, g)
            sp.wait_ge(s_out, 16 * NG)

        @block.gpsimd
        def _(pool):
            nc.gpsimd.memset(ones[:, :], 1.0).then_inc(s_ones, 1)
            nc.gpsimd.memset(onesC[:, :], 1.0)
            nc.gpsimd.memset(big[:, :], BIG)
            nc.gpsimd.memset(zrow[:, :], 0.0)
            nc.gpsimd.memset(hrow[:, :, DEN:DEN + 1], 1.0)
            nc.gpsimd.iota(iota_s[:, :], [[1, U * P]], base=0, channel_multiplier=0, allow_small_or_imprecise_dtypes=True)
            nc.gpsimd.iota(iota_turn[:, :], [[P * U, TURNS]], base=0, channel_multiplier=0,
                           allow_small_or_imprecise_dtypes=True)
            nc.gpsimd.iota(place_i[:, :], [[P, U]], base=0, channel_multiplier=1)
            nc.gpsimd.memset(group_row[:, :], float(-PADROW))
            nc.gpsimd.memset(V[:, :].rearrange("p (r w) -> p r w", w=HW)[:, :, DEN:DEN + 1], 1.0)
            pool.wait_ge(s_ones, 1)
            for target, base, op in ((ident, 0, ALU.is_equal), (before, 0, ALU.is_gt), (shift, -1, ALU.is_equal)):
                nc.gpsimd.affine_select(out=target[:, :], in_=ones[:, :], pattern=[[1, P]], compare_op=op,
                                        fill=0.0, base=base, channel_multiplier=-1)
            nc.gpsimd.affine_select(out=local[:, C:C + 1], in_=ones[:, 0:1], pattern=[[0, 1]], compare_op=ALU.is_gt,
                                    fill=0.0, base=0, channel_multiplier=1).then_inc(s_const, 1)

            def fetch(layer, k, total):
                at = listed(pool, k, total)
                for u in range(U):
                    pool.wait_ge(s_feed, k * U + u + 1)
                    apart(pool)
                    nc.gpsimd.tensor_copy(idx[:, u, :], lists[:, bass.ds(at * U + u, 1), :].rearrange("p o t -> p (o t)")
                                          ).then_inc(s_idx, 1)
                    pool.wait_ge(s_idx, k * U + u + 1)
                    apart(pool)
                    pool.indirect_dma_start(
                        out=st_feat[:, u, 0:(D if layer == 0 else HW)], out_offset=None,
                        in_=(feat if layer == 0 else table),
                        in_offset=bass.IndirectOffsetOnAxis(idx[:, u, 0:1].bitcast(U32), 0)).then_inc(s_gf[u], 16)
                    if layer == 0:
                        pool.indirect_dma_start(
                            out=st_mask[:, u, :], out_offset=None, in_=adjT,
                            in_offset=bass.IndirectOffsetOnAxis(idx[:, u, 1:2].bitcast(U32), 0)).then_inc(s_gm[u], 16)

            def feed(layer, k):
                slot = ring(pool, k)
                w = D if layer == 0 else HW
                for u in range(U):
                    pool.wait_ge(s_pv, k * U + u + 1)
                    pool.wait_ge(s_gf[u], 16 * k + 16)
                    apart(pool)
                    last = nc.gpsimd.tensor_copy(V[:, bass.ds((slot + u) * HW, w)], st_feat[:, u, 0:w])
                    if layer == 0:
                        pool.wait_ge(s_gm[u], 16 * k + 16)
                        apart(pool)
                        last = nc.gpsimd.tensor_copy(F[:, bass.ds((slot + u) * G, G)], st_mask[:, u, :])
                    last.then_inc(s_feed, 1)

            pool.sem_inc(s_feed, U)
            with pool.Fori(0, NG) as g:
                pool.wait_ge(s_list, g + 1)
                apart(pool)
                lo, hi = rounds(pool, 0, g)
                with pool.Fori(lo, hi) as k:
                    fetch(0, k, None)
                    feed(0, k)
            pool.wait_ge(s_st, 32 * NG + 32)
            total = pool.value_load(bounds[0:1, NG:NG + 1], min_val=1, max_val=NG * TURNS)
            end = pool.value_load(bounds[0:1, 2 * NG + 1:2 * NG + 2], min_val=1, max_val=2 * NG * TURNS)
            with pool.Fori(total, end) as k:
                fetch(1, k, total)
                feed(1, k)

        @block.scalar
        def _(act):
            act.sem_inc(s_piece_a, RING)
            act.sem_inc(s_mst, 16)
            act.sem_inc(s_st, 32)
            act.wait_ge(s_wx, 1)
            nc.scalar.copy(w1x[:, COLT:COLT + 1], ps_X[:, 1:2])
            nc.scalar.mul(w1x[:, COLTS:COLTS + 1], ps_X[:, 1:2], SLOPE)
            nc.scalar.copy(w1x[:, ROWT:ROWT + 1], ps_X[:, 0:1]).then_inc(s_w1x, 1)
            act.wait_ge(s_mean, 1)
            nc.scalar.mul(mean0[:, :], ps_X[:, 0:D], 1.0 / N).then_inc(s_meanc, 1)

            def scan(g, stage):
                if stage == 0:
                    act.wait_ge(s_occ_free, g + 1)
                for n in range(*STAGES[stage]):
                    act.wait_ge(s_scan[n % RING], (g * PER_RING + n // RING) * 16 + 16)
                    for c in range(V_COLS, PC):
                        last = nc.scalar.activation(scan_buf[:, n % RING, c, :], scan_buf[:, n % RING, c, :], ACT.Relu,
                                                    accum_out=occ[:, n * PC + c:n * PC + c + 1])
                    last.then_inc(s_piece_a, 1)

            def exponentials(lo, hi, scale):
                with act.Fori(lo, hi) as k:
                    slot = ring(act, k)
                    act.wait_ge(s_dif, k + 2)
                    for u in range(U):
                        act.wait_ge(s_pv, k * U + u + 1 + C - U)
                        nc.scalar.activation(prob[:, u, :], S[:, bass.ds((slot + u) * G, G)], ACT.Exp,
                                             scale=scale).then_inc(s_p, 1)

            def scores(g):
                act.wait_ge(s_list, g + 1)
                apart(act)
                lo, hi = rounds(act, 0, g)
                act.wait_ge(s_pre, g + 1)
                nc.scalar.copy(qT[:, :], ps_B[:, :]).then_inc(s_q, 1)
                with act.Fori(lo, hi) as k:
                    slot = ring(act, k)
                    at = listed(act, k, None)
                    act.wait_ge(s_feed, k * U + 2 * U)
                    nc.scalar.copy(kst[:, :, :],
                                   V[:, bass.ds(slot * HW, U * HW)].rearrange("p (u w) -> p u w", u=U)[:, :, 0:D]
                                   ).then_inc(s_kst, 1)
                    act.wait_ge(s_mst, 16 * k + 16)
                    nc.scalar.activation(fill[:, :, :], F[:, bass.ds(slot * G, U * G)].rearrange("p (u i) -> p u i", u=U),
                                         ACT.Relu, scale=-BIG, bias=big[:, 0:1]).then_inc(s_fill, 1)
                    act.wait_ge(s_tr, k + 1)
                    nc.scalar.copy(kT[:, :, :], ps_T[:, :, :]).then_inc(s_kt, 1)
                    act.wait_ge(s_fill, k + 1)
                    act.dma_start(masks[bass.ds(at, 1), :, :, :].rearrange("t p u i -> (t p) u i"),
                                  fill[:, :, :]).then_inc(s_mst, 16)
                    act.wait_ge(s_raw, k + 1)
                    nc.scalar.copy(S[:, bass.ds(slot * G, U * G)].rearrange("p (u i) -> p u i", u=U),
                                   ps_S[:, :, 0:G]).then_inc(s_sc, 1)

            def new_rows(g):
                act.wait_ge(s_xT, g + 1)
                nc.scalar.activation(xnT[:, :], ps_X[:, 0:G], ACT.Copy,
                                     accum_out=xsum[:, bass.ds(g, 1)]).then_inc(s_xTc, 1)
                act.wait_ge(s_h, g + 1)
                act.wait_ge(s_st, 32 * g + 32)
                hx = ps_X[:, 0:SUB * WX].rearrange("p (s w) -> p s w", s=SUB)
                nc.scalar.copy(hrow[:, :, 0:D], hx[:, :, 0:D])
                nc.scalar.copy(hrow[:, :, COLT:HW], hx[:, :, COLT:HW])
                nc.scalar.copy(s1col[:, bass.ds(g * SUB, SUB)], hx[:, :, ROWT:WX].rearrange("p s o -> p (s o)")
                               ).then_inc(s_hc, 1)
                act.wait_ge(s_hc, g + 1)
                act.dma_start(table_rows[bass.ds(g, 1), :, :, :].rearrange("g p s d -> (g p) s d"),
                              hrow[:, :, :]).then_inc(s_st, 16)
                act.dma_start(x1_rows[bass.ds(g, 1), :, :, :].rearrange("g p s d -> (g p) s d"),
                              xn[:, :, :]).then_inc(s_st, 16)

            def attend1(g):
                lo, hi = rounds(act, 1, g)
                act.wait_ge(s_mb, NG + g + 1)
                with act.Fori(lo, hi) as k:
                    slot = ring(act, k)
                    for u in range(U):
                        last = nc.scalar.activation(S[:, bass.ds((slot + u) * G, G)], ps_S[:, 0, 0:G], ACT.Identity,
                                                    bias=V[:, bass.ds((slot + u) * HW + COLTS, 1)])
                    last.then_inc(s_sc, 1)
                exponentials(lo, hi, 1.0)

            def attend0(g, scans, scores_next):
                if scans:
                    scan(g + 2, 0)
                exponentials(*rounds(act, 0, g), 1.0 / TEMPERATURE)
                if scans:
                    scan(g + 2, 1)
                if scores_next:
                    scores(g + 1)
                new_rows(g)
                if scans:
                    scan(g + 2, 2)

            for g in range(2):
                for stage in range(len(STAGES)):
                    scan(g, stage)
            scores(0)
            with act.Fori(0, NG - 2) as g:
                attend0(g, True, True)
            attend0(NG - 2, False, True)
            attend0(NG - 1, False, False)
            act.wait_ge(s_mean, 2)
            nc.scalar.copy(mean1[:, :], ps_X[:, 0:D]).then_inc(s_meanc, 1)
            with act.Fori(0, NG) as g:
                attend1(g)
            for g in range(NG):
                act.wait_ge(s_xn, NG + g + 1)
                act.dma_start(out_rows[g], y_all[:, g * G:(g + 1) * G].rearrange("p (s d) -> p s d", s=SUB)
                              ).then_inc(s_out, 16)
            act.wait_ge(s_out, 16 * NG)

        @block.tensor
        def _(pe):
            pe.sem_inc(s_pv, C)
            pe.wait_ge(s_const, 1)
            pe.wait_ge(s_load, 64)
            nc.tensor.matmul(ps_X[:, 0:2], w1T_sb[:, :], a_sb[:, :], start=True, stop=True).then_inc(s_wx, 1)
            pe.wait_ge(s_w1x, 1)
            pe.wait_ge(s_feat, 16)
            for c in range(C):
                last = nc.tensor.matmul(ps_X[:, 0:D], ones[:, :], feat_all[:, c * D:(c + 1) * D],
                                        start=(c == 0), stop=(c == C - 1))
            last.then_inc(s_mean, 1)

            def compact(g):
                pe.wait_ge(s_tot, g + 1)
                count = prefix[:, C - 1:C]
                nc.tensor.matmul(ps_L[:, 0:C], steps[:, :], prefix[:, :], start=True, stop=True)
                nc.tensor.matmul(ps_L[:, C:C + 1], shift[:, :], count, start=True, stop=True)
                nc.tensor.matmul(ps_L[:, C + 1:C + 2], before[:, :], count, start=True, stop=True)
                nc.tensor.matmul(ps_L[:, C + 2:C + 3], ones[:, :], count, start=True, stop=True).then_inc(s_off, 1)
                pe.wait_ge(s_bound, g + 1)
                apart(pe)
                lo, hi = rounds(pe, 0, g)
                with pe.Fori(lo, hi) as k:
                    pe.wait_ge(s_reach, k + 1)
                    for u in range(U):
                        last = nc.tensor.matmul(ps_L[:, 64 * (u + 1):64 * (u + 1) + LOC],
                                                reached[:, u * P:(u + 1) * P], local[:, :], start=True, stop=True)
                    last.then_inc(s_pick, 1)

            def transpose_maximum(gg):
                pe.wait_ge(s_max, gg + 1)
                for s in range(SUB):
                    last = nc.tensor.transpose(ps_B[:, s * P:(s + 1) * P], M[:, s * P:(s + 1) * P], ident[:, :])
                last.then_inc(s_mT, 1)

            def zero_sums(gg):
                pe.wait_ge(s_O_free, gg + 1)
                nc.tensor.matmul(ps_O[:, :, :].rearrange("p s d -> p (s d)"), zrow[:, 0:P], zrow[:, 0:SUB * (D + 1)],
                                 start=True, stop=False, skip_group_check=True)

            def broadcast(layer, gg):
                pe.wait_ge(s_diag, gg + 1)
                if layer == 1:
                    nc.tensor.matmul(ps_S[:, 0, 0:G], ones[:, :], diag_flat[:, :, :].rearrange("p s i -> p (s i)"),
                                     start=True, stop=True)
                nc.tensor.matmul(ps_B[:, :], ones[:, :], diag[:, :, :].rearrange("p s i -> p (s i)"),
                                 start=True, stop=True).then_inc(s_mb, 1)

            def sums(lo, hi):
                with pe.Fori(lo, hi) as k:
                    slot = ring(pe, k)
                    for u in range(U):
                        pe.wait_ge(s_p, k * U + u + 1)
                        for s in range(SUB):
                            last = nc.tensor.matmul(ps_O[:, s, :], prob[:, u, s * P:(s + 1) * P],
                                                    V[:, bass.ds((slot + u) * HW, D + 1)], start=False, stop=False,
                                                    skip_group_check=True)
                        last.then_inc(s_pv, 1)
                nc.tensor.matmul(ps_O[:, :, :].rearrange("p s d -> p (s d)"), zrow[:, 0:P], zrow[:, 0:SUB * (D + 1)],
                                 start=False, stop=True, skip_group_check=True).then_inc(s_O, 1)

            def scores(g):
                lo, hi = rounds(pe, 0, g)
                pe.wait_ge(s_dif, lo + 1)
                pe.wait_ge(s_small, 32 * g + 32)
                nc.tensor.matmul(ps_B[:, :], w0_sb[:, :], xT_sb[:, bass.ds((g % 2) * G, G)],
                                 start=True, stop=True).then_inc(s_pre, 1)
                pe.wait_ge(s_q, g + 1)
                apart(pe)
                with pe.Fori(lo, hi) as k:
                    pe.wait_ge(s_kst, k + 1)
                    for u in range(U):
                        last = nc.tensor.transpose(ps_T[:, u, :], kst[:, u, :], ident[:, :])
                    last.then_inc(s_tr, 1)
                    pe.wait_ge(s_fill, k + 1)
                    pe.wait_ge(s_kt, k + 1)
                    for u in range(U):
                        nc.tensor.matmul(ps_S[:, u, 0:G], kT[:, u, :], qT[:, :], start=True, stop=False)
                        last = nc.tensor.matmul(ps_S[:, u, 0:G], mask_w[:, :], fill[:, u, :], start=False, stop=True)
                    last.then_inc(s_raw, 1)

            def new_rows(g):
                pe.wait_ge(s_xn, g + 1)
                for s in range(SUB):
                    last = nc.tensor.transpose(ps_X[:, s * P:(s + 1) * P], xn[:, s, :], ident[:, :])
                last.then_inc(s_xT, 1)
                pe.wait_ge(s_xTc, g + 1)
                for s in range(SUB):
                    last = nc.tensor.matmul(ps_X[:, s * WX:(s + 1) * WX], xnT[:, s * P:(s + 1) * P], w1x[:, :],
                                            start=(s == 0), stop=True, skip_group_check=True)
                last.then_inc(s_h, 1)

            def attend0(g, compacts, scores_next):
                transpose_maximum(g)
                zero_sums(g)
                broadcast(0, g)
                sums(*rounds(pe, 0, g))
                if scores_next:
                    scores(g + 1)
                new_rows(g)
                if compacts:
                    compact(g + 2)

            def attend1(g):
                zero_sums(g + NG)
                broadcast(1, g + NG)
                sums(*rounds(pe, 1, g))

            pe.wait_ge(s_vconst, 1)
            pe.wait_ge(s_meanc, 1)
            compact(0)
            compact(1)
            scores(0)
            with pe.Fori(0, NG - 2) as g:
                attend0(g, True, True)
            attend0(NG - 2, False, True)
            attend0(NG - 1, False, False)
            pe.wait_ge(s_hc, NG)
            pe.wait_ge(s_xmean, 1)
            nc.tensor.matmul(ps_X[:, 0:D], diag[:, 0, :], w1x[:, 0:D], start=True, stop=True).then_inc(s_mean, 1)
            transpose_maximum(NG)
            with pe.Fori(0, NG - 1) as g:
                attend1(g)
                transpose_maximum(g + NG + 1)
            attend1(NG - 1)

        @block.vector
        def _(dve):
            dve.sem_inc(s_piece_v, RING)
            dve.sem_inc(s_occ_free, 1)
            dve.sem_inc(s_small_free, 2)
            dve.sem_inc(s_O_free, 1)
            dve.sem_inc(s_dif, 1)
            nc.vector.memset(turn_sum[:, :], 0.0)
            nc.vector.memset(bounds[:, :], 0)
            nc.vector.memset(w1x[:, DEN:DEN + 1], 0.0)
            dve.wait_ge(s_const, 1)
            nc.vector.tensor_tensor(steps[:, :], ident[:, :], shift[:, :], ALU.subtract)
            nc.vector.tensor_scalar(mask_w[:, :], ident[:, :], -1.0, None, ALU.mult).then_inc(s_vconst, 1)

            def scan(g, stage):
                for n in range(*STAGES[stage]):
                    dve.wait_ge(s_scan[n % RING], (g * PER_RING + n // RING) * 16 + 16)
                    nc.vector.tensor_reduce(occ[:, n * PC:n * PC + V_COLS], scan_buf[:, n % RING, 0:V_COLS, :],
                                            AX.X, ALU.max).then_inc(s_piece_v, 1)

            def compact(g):
                dve.drain()
                dve.wait_ge(s_piece_a, g * PIECES + PIECES + RING)
                nc.vector.tensor_scalar(present[:, :], occ[:, :], 0.0, None, ALU.is_gt).then_inc(s_occ_free, 1)
                dve.drain()
                nc.vector.tensor_tensor_scan(prefix[:, :], onesC[:, :], present[:, :], 0.0, ALU.mult, ALU.add
                                             ).then_inc(s_tot, 1)
                nc.vector.tensor_copy(place[:, :], place0[:, :])
                dve.wait_ge(s_off, g + 1)
                nc.vector.tensor_copy(offs[:, :], ps_L[:, C + 1:C + 3])
                nc.vector.tensor_copy(local[:, 0:C], ps_L[:, 0:C])
                nc.vector.tensor_copy(local[:, C + 1:C + 2], ps_L[:, C:C + 1])
                dve.drain()
                nc.vector.tensor_scalar(turn_flags[:, :], iota_turn[:, :], offs[0:1, 1:2], None, ALU.is_lt)
                nc.vector.tensor_copy(first[:, :], offs[:, 0:1])
                dve.drain()
                nc.vector.tensor_reduce(turn_n[:, :], turn_flags[:, :], AX.X, ALU.add)
                dve.drain()
                nc.vector.scalar_tensor_tensor(out=turn_sum[:, :], in0=turn_n[:, :], scalar=1.0,
                                               in1=turn_sum[:, :], op0=ALU.max, op1=ALU.add)
                dve.drain()
                nc.vector.tensor_copy(bounds[0:1, bass.ds(g + 1, 1)], turn_sum[:, :]).then_inc(s_bound, 1)
                dve.wait_ge(s_bound, g + 1)
                apart(dve)
                lo, hi = rounds(dve, 0, g)
                with dve.Fori(lo, hi) as k:
                    at = listed(dve, k, None)
                    nc.vector.tensor_scalar(reached[:, :], iota_s[:, :], first[:, 0:1], None, ALU.is_ge
                                            ).then_inc(s_reach, 1)
                    nc.vector.tensor_scalar(real[:, :], place[:, :], offs[:, 1:2], None, ALU.is_lt)
                    nc.vector.tensor_scalar(first[:, :], first[:, :], float(-U * P), None, ALU.add)
                    dve.wait_ge(s_pick, k + 1)
                    pick = ps_L[:, 64:64 * (U + 1)].rearrange("p (u w) -> p u w", u=U)
                    nc.vector.tensor_tensor(rank[:, :], place[:, :], pick[:, :, C + 1:C + 2].rearrange("p u o -> p (u o)"),
                                            ALU.subtract)
                    dve.drain()
                    nc.vector.tensor_tensor(ahead[:, :, :], pick[:, :, 0:C],
                                            rank[:, :].unsqueeze(2).to_broadcast([P, U, C]), ALU.is_le)
                    nc.vector.tensor_scalar(place[:, :], place[:, :], float(U * P), None, ALU.add)
                    dve.drain()
                    nc.vector.tensor_reduce(ccol[:, :], ahead[:, :, :], AX.X, ALU.add)
                    dve.drain()
                    nc.vector.scalar_tensor_tensor(out=jcol[:, :], in0=pick[:, :, C:C + 1].rearrange("p u o -> p (u o)"),
                                                   scalar=float(C), in1=ccol[:, :], op0=ALU.mult, op1=ALU.add)
                    dve.drain()
                    nc.vector.scalar_tensor_tensor(out=mrow[:, :], in0=jcol[:, :], scalar=group_row[:, 0:1],
                                                   in1=real[:, :], op0=ALU.add, op1=ALU.mult)
                    nc.vector.tensor_scalar(lists[:, bass.ds(at * U, U), 0], jcol[:, :], float(N - 1), None, ALU.min)
                    dve.drain()
                    nc.vector.tensor_scalar(lists[:, bass.ds(at * U, U), 1], mrow[:, :], float(PADROW), None, ALU.add)
                dve.drain()
                nc.vector.tensor_scalar(group_row[:, :], group_row[:, :], float(N), None, ALU.add
                                        ).then_inc(s_list, 1)

            def rsqrt(n):
                dve.drain()
                nc.vector.tensor_scalar(half[:, 0:n], var[:, 0:n].bitcast(I32), 1, None, ALU.logical_shift_right)
                dve.drain()
                nc.vector.tensor_scalar(rstd[:, 0:n].bitcast(I32), half[:, 0:n], -1.0, float(0x5F3759DF),
                                        ALU.mult, ALU.add)
                for _ in range(3):
                    dve.drain()
                    nc.vector.tensor_tensor(rsq[:, 0:n], rstd[:, 0:n], rstd[:, 0:n], ALU.mult)
                    dve.drain()
                    nc.vector.scalar_tensor_tensor(out=rsq[:, 0:n], in0=rsq[:, 0:n], scalar=-0.5, in1=var[:, 0:n],
                                                   op0=ALU.mult, op1=ALU.mult)
                    dve.drain()
                    nc.vector.scalar_tensor_tensor(out=rstd[:, 0:n], in0=rsq[:, 0:n], scalar=1.5, in1=rstd[:, 0:n],
                                                   op0=ALU.add, op1=ALU.mult)
                dve.drain()

            def diagonal(target, col):
                return nc.vector.tensor_tensor(target[:, :, :], ident[:, :].unsqueeze(1).to_broadcast([P, SUB, P]),
                                               col.unsqueeze(2).to_broadcast([P, SUB, P]), ALU.mult)

            def attended(layer, g, target):
                dve.wait_ge(s_O, g + layer * NG + 1)
                nc.vector.tensor_scalar(rden[:, :], ps_O[:, :, DEN:DEN + 1].rearrange("p s o -> p (s o)"), 0.5, None,
                                        ALU.max)
                dve.drain()
                nc.vector.reciprocal(rden[:, :], rden[:, :])
                dve.drain()
                nc.vector.tensor_tensor(rdf[:, :], rden[:, :], full[:, :], ALU.mult)
                dve.drain()
                if layer == 0:
                    dve.wait_ge(s_small, 32 * g + 32)
                else:
                    dve.wait_ge(s_small, 32 * NG + 16 * g + 16)
                    dve.wait_ge(s_meanc, 2)
                for s in range(SUB):
                    last = nc.vector.scalar_tensor_tensor(out=y[:, s, :], in0=ps_O[:, s, 0:D], scalar=rdf[:, s:s + 1],
                                                          in1=xres[:, bass.ds((g % 2) * G + s * D, D)],
                                                          op0=ALU.mult, op1=ALU.add)
                last.then_inc(s_small_free, 1)
                dve.drain()
                for s in range(SUB):
                    last = nc.vector.scalar_tensor_tensor(out=target(s), in0=(mean0 if layer == 0 else mean1)[:, :],
                                                          scalar=empty[:, s:s + 1], in1=y[:, s, :],
                                                          op0=ALU.mult, op1=ALU.add)
                last.then_inc(s_O_free, 1)
                dve.drain()
                for s in range(SUB):
                    nc.vector.bn_stats(stats[:, s, :], target(s))
                dve.drain()
                for s in range(SUB):
                    nc.vector.bn_aggr(mv[:, s, :], stats[:, s, :])
                dve.drain()

            def maximum_ready():
                dve.drain()
                nc.vector.tensor_copy(mcol[:, 0:1], M[:, 0:1]).then_inc(s_max, 1)

            def row_maximum(layer, g):
                dve.wait_ge(s_mT, g + layer * NG + 1)
                nc.vector.tensor_reduce(mcol[:, :], ps_B[:, :].rearrange("p (s q) -> p s q", s=SUB), AX.X,
                                        ALU.max if layer == 0 else ALU.min)
                dve.drain()

            def attend0(g, scans):
                lo, hi = rounds(dve, 0, g)
                nc.vector.memset(M[:, :], LEAST)
                with dve.Fori(lo, hi) as k:
                    slot = ring(dve, k)
                    for u in range(U):
                        dve.drain()
                        if u == 0:
                            dve.wait_ge(s_sc, k + 1)
                        nc.vector.tensor_tensor(M[:, :], M[:, :], S[:, bass.ds((slot + u) * G, G)], ALU.max)
                maximum_ready()
                row_maximum(0, g)
                diagonal(diag, mcol[:, :]).then_inc(s_diag, 1)
                nc.vector.tensor_scalar(empty[:, :], mcol[:, :], -BIG / 2, None, ALU.is_lt)
                nc.vector.tensor_scalar(full[:, :], mcol[:, :], -BIG / 2, None, ALU.is_ge)
                if scans:
                    scan(g + 2, 0)
                dve.wait_ge(s_mb, g + 1)
                apart(dve)
                with dve.Fori(lo, hi) as k:
                    turn = S[:, bass.ds(ring(dve, k) * G, U * G)].rearrange("p (u i) -> p u i", u=U)
                    nc.vector.tensor_tensor(turn, turn, ps_B[:, :].unsqueeze(1).to_broadcast([P, U, G]), ALU.subtract
                                            ).then_inc(s_dif, 1)
                if scans:
                    scan(g + 2, 1)
                attended(0, g, lambda s: y[:, s, :])
                nc.vector.tensor_scalar(var[:, 0:SUB], mv[:, :, 1:2].rearrange("p s o -> p (s o)"), EPS, None, ALU.add)
                rsqrt(SUB)
                dve.wait_ge(s_st, 32 * g + 32)
                for s in range(SUB):
                    last = nc.vector.tensor_scalar(xn[:, s, :], y[:, s, :], mv[:, s, 0:1], rstd[:, s:s + 1],
                                                   ALU.subtract, ALU.mult)
                last.then_inc(s_xn, 1)
                if scans:
                    scan(g + 2, 2)
                    compact(g + 2)

            def greatest_terms(g):
                lo, hi = rounds(dve, 1, g)
                nc.vector.memset(M[:, :], -LEAST)
                with dve.Fori(lo, hi) as k:
                    slot = ring(dve, k)
                    for u in range(U):
                        dve.drain()
                        if u == 0:
                            dve.wait_ge(s_mst, k * 16 + 32)
                        dve.wait_ge(s_feed, k * U + u + 1 + U)
                        nc.vector.scalar_tensor_tensor(out=M[:, :], in0=F[:, bass.ds((slot + u) * G, G)],
                                                       scalar=V[:, bass.ds((slot + u) * HW + COLT, 1)],
                                                       in1=M[:, :], op0=ALU.subtract, op1=ALU.min)
                maximum_ready()

            def exponents1(g):
                gg = g + NG
                row_maximum(1, g)
                s1 = s1col[:, bass.ds(g * SUB, SUB)]
                nc.vector.tensor_tensor(mrow_t[:, :], s1, mcol[:, :], ALU.subtract)
                nc.vector.tensor_scalar(empty[:, :], mcol[:, :], BIG / 2, None, ALU.is_gt)
                nc.vector.tensor_scalar(full[:, :], mcol[:, :], BIG / 2, None, ALU.is_le)
                dve.drain()
                nc.vector.scalar_tensor_tensor(out=mrow_t[:, :], in0=mrow_t[:, :], scalar=SLOPE, in1=mrow_t[:, :],
                                               op0=ALU.mult, op1=ALU.max)
                dve.drain()
                nc.vector.tensor_tensor(rterm[:, 0, :], s1, mrow_t[:, :], ALU.subtract)
                nc.vector.scalar_tensor_tensor(out=rterm[:, 1, :], in0=s1, scalar=SLOPE, in1=mrow_t[:, :],
                                               op0=ALU.mult, op1=ALU.subtract)
                dve.drain()
                diagonal(diag_flat, rterm[:, 1, :])
                diagonal(diag, rterm[:, 0, :]).then_inc(s_diag, 1)
                dve.wait_ge(s_mb, gg + 1)
                apart(dve)
                lo, hi = rounds(dve, 1, g)
                with dve.Fori(lo, hi) as k:
                    slot = ring(dve, k)
                    dve.wait_ge(s_sc, k + 1)
                    for u in range(U):
                        at = bass.ds((slot + u) * G, G)
                        nc.vector.scalar_tensor_tensor(out=S[:, at], in0=ps_B[:, :],
                                                       scalar=V[:, bass.ds((slot + u) * HW + COLT, 1)],
                                                       in1=S[:, at], op0=ALU.add, op1=ALU.max)
                    dve.drain()
                    turn = bass.ds(slot * G, U * G)
                    nc.vector.tensor_tensor(S[:, turn], S[:, turn], F[:, turn], ALU.subtract).then_inc(s_dif, 1)

            def new_rows1(g):
                attended(1, g, lambda s: y_all[:, bass.ds(g * G + s * D, D)])
                nc.vector.tensor_copy(mvs[:, bass.ds(g * SUB, SUB), :], mv[:, :, :])

            nc.vector.tensor_copy(place0[:, :], place_i[:, :])
            dve.drain()
            for g in range(2):
                for stage in range(len(STAGES)):
                    scan(g, stage)
                compact(g)
            with dve.Fori(0, NG - 2) as g:
                attend0(g, True)
            attend0(NG - 2, False)
            nc.vector.tensor_scalar(bounds[0:1, NG + 1:2 * NG + 2], bounds[0:1, 0:NG + 1], turn_sum[0:1, 0:1], None,
                                    ALU.add)
            attend0(NG - 1, False)
            dve.wait_ge(s_xTc, NG)
            nc.vector.tensor_reduce(xmean[:, :], xsum[:, :], AX.X, ALU.add)
            dve.drain()
            nc.vector.tensor_scalar(diag[:, 0, :], ones[:, :], xmean[:, 0:1], 1.0 / N, ALU.mult, ALU.mult
                                    ).then_inc(s_xmean, 1)
            dve.wait_ge(s_meanc, 2)
            greatest_terms(0)
            with dve.Fori(0, NG - 1) as g:
                exponents1(g)
                greatest_terms(g + 1)
                new_rows1(g)
            exponents1(NG - 1)
            new_rows1(NG - 1)
            dve.drain()
            nc.vector.tensor_scalar(var[:, :], mvs[:, :, 1:2].rearrange("p s o -> p (s o)"), EPS, None, ALU.add)
            rsqrt(NG * SUB)
            for g in range(NG):
                for s in range(SUB):
                    n = g * SUB + s
                    rows = y_all[:, n * D:(n + 1) * D]
                    last = nc.vector.tensor_scalar(rows, rows, mvs[:, n, 0:1], rstd[:, n:n + 1],
                                                   ALU.subtract, ALU.mult)
                last.then_inc(s_xn, 1)


def kernel(**inputs):
    import numpy as np
    import concourse.bacc as bacc
    from concourse import mybir as mb
    from concourse.bass_utils import run_bass_kernel_spmd

    x = np.ascontiguousarray(inputs["x"])
    adj = np.asarray(inputs["adj"])
    n, d = x.shape
    arrays = {
        "x": x,
        "xT": np.ascontiguousarray(x.T),
        "adjT": np.concatenate([adj.reshape(n // G, G, n).transpose(0, 2, 1).reshape(-1, G),
                                np.zeros((1, G), adj.dtype)]),
        "feat": np.ascontiguousarray(inputs["L0_gnn_input"]),
        "w0": np.ascontiguousarray(inputs["L0_gnn_weight"]),
        "w1": np.ascontiguousarray(inputs["L1_gnn_W"]),
        "w1T": np.ascontiguousarray(np.asarray(inputs["L1_gnn_W"]).T),
        "a": np.ascontiguousarray(np.asarray(inputs["L1_gnn_a"]).reshape(2, d).T),
    }
    nc = bacc.Bacc("TRN2", target_bir_lowering=False, num_devices=1)
    args = [nc.dram_tensor(f"in_{k}", v.shape, mb.dt.from_np(v.dtype), kind="ExternalInput").ap()
            for k, v in arrays.items()]
    x1_dram = nc.dram_tensor("x1_dram", (n, d), F32, kind="Internal").ap()
    table = nc.dram_tensor("table", (n, d + 3), F32, kind="Internal").ap()
    masks = nc.dram_tensor("masks", (n // G * (n // P // U), P, U, G), BF16, kind="Internal").ap()
    out = nc.dram_tensor("out_x", (n, d), F32, kind="ExternalOutput").ap()
    graph_attention_kernel(nc, *args, x1_dram, table, masks, out)
    r = run_bass_kernel_spmd(nc, [{f"in_{k}": v for k, v in arrays.items()}], core_ids=[0])
    return r.results[0]["out_x"]
```

```python
from contextlib import ExitStack, contextmanager

import concourse.bass as bass
from concourse import mybir

P = 128
U = 3
W = 2 * U
SUB = 3
G = SUB * P
PIECES = 12
AHEAD = 3
RING = 3
V_STAGES = ((0, 1), (1, 2), (2, 3), (3, 6), (6, 9))
A_STAGES = ((9, 10), (10, 11), (11, 12))
V_PIECES = V_STAGES[-1][-1]
A_PIECES = PIECES - V_PIECES
TEMPERATURE = 0.07
SLOPE = 0.01
EPS = 1e-5
BIG = 2.0 ** 60
LEAST = -3.0e38

ALU = mybir.AluOpType
ACT = mybir.ActivationFunctionType
AX = mybir.AxisListType
F32 = mybir.dt.float32
BF16 = mybir.dt.bfloat16
I32 = mybir.dt.int32
U32 = mybir.dt.uint32


def graph_attention_kernel(nc, x, xT, adjT, feat, w0, w1, w1T, a, x1_dram, table, masks, out):
    N, D = feat.shape
    NG = N // G
    C = N // P
    PC = C // PIECES
    PER_RING = V_PIECES // RING
    TURNS = C // U
    DEN = D
    COLT, COLTS = D + 1, D + 2
    LATE = 2
    HW = D + 3
    ROWT = D + 3
    WX = D + 4
    PADROW = NG * N
    LOC = C + 2

    scan_src = adjT[0:NG * N, :].rearrange("(g p c) i -> g p c i", c=C, p=P)
    x_rows = x.rearrange("(g s p) d -> g p s d", s=SUB, p=P)
    x1_rows = x1_dram.rearrange("(g s p) d -> g p s d", s=SUB, p=P)
    out_rows = out.rearrange("(g s p) d -> g p s d", s=SUB, p=P)
    table_rows = table.rearrange("(g s p) d -> g p s d", s=SUB, p=P)
    xT_groups = xT.rearrange("d (g i) -> g d i", i=G)

    with ExitStack() as ctx:
        def sb(name, shape, dt=F32):
            return ctx.enter_context(nc.sbuf_tensor(name, shape, dt))

        def pb(name, shape, dt=F32):
            return ctx.enter_context(nc.psum_tensor(name, shape, dt))

        def sem(name):
            return ctx.enter_context(nc.semaphore(name))

        ident = sb("ident", [P, P])
        before = sb("before", [P, P])
        shift = sb("shift", [P, P])
        steps = sb("steps", [P, P])
        ones = sb("ones", [P, P])
        mask_w = sb("mask_w", [P, P], BF16)
        zrow = sb("zrow", [1, 512], BF16)
        big = sb("big", [P, 1])
        iota_s = sb("iota_s", [P, U * P])
        iota_turn = sb("iota_turn", [1, TURNS])
        onesC = sb("onesC", [P, C])
        w0_sb = sb("w0_sb", [P, D])
        w1x = sb("w1x", [P, WX])
        w1T_sb = sb("w1T_sb", [P, D])
        a_sb = sb("a_sb", [P, 2])
        mean0 = sb("mean0", [P, D])
        mean1 = sb("mean1", [P, D])
        scan_buf = sb("scan_buf", [P, RING + 1, PC, G], I32)
        occ = sb("occ", [P, C])
        present = sb("present", [P, C])
        prefix = sb("prefix", [P, C])
        local = sb("local", [P, LOC], BF16)
        offs = sb("offs", [P, 2])
        first = sb("first", [P, 1])
        reached = sb("reached", [P, W * P], BF16)
        place_i = sb("place_i", [P, W], I32)
        place0 = sb("place0", [P, W])
        place = sb("place", [P, W])
        real = sb("real", [P, W])
        rank = sb("rank", [P, W])
        ahead = sb("ahead", [P, W, C], BF16)
        ccol = sb("ccol", [P, W])
        jcol = sb("jcol", [P, W])
        mrow = sb("mrow", [P, W])
        group_row = sb("group_row", [P, 1])
        lists = sb("lists", [P, (NG + 1) * C, 2], I32)
        turn_flags = sb("turn_flags", [1, TURNS])
        turn_n = sb("turn_n", [1, 2])
        turn_sum = sb("turn_sum", [1, 2])
        bounds = sb("bounds", [1, 3 * (NG + 1)], I32)
        idx = sb("idx", [P, U, 2], I32)
        st_feat = sb("st_feat", [P, U, HW])
        st_mask = sb("st_mask", [P, U, G], I32)
        V = sb("V", [P, C * HW])
        F = sb("F", [P, C * G], BF16)
        S = sb("S", [P, C * G])
        kst = sb("kst", [P, U, P])
        kT = sb("kT", [P, U, P])
        fill = sb("fill", [P, U, G], BF16)
        prob = sb("prob", [P, U, G])
        M = sb("M", [P, G])
        mcol = sb("mcol", [P, SUB])
        mrow_t = sb("mrow_t", [P, SUB])
        rterm = sb("rterm", [P, 2, SUB])
        diag = sb("diag", [P, SUB, P])
        xT_sb = sb("xT_sb", [P, 2 * G])
        xres = sb("xres", [P, 2 * G])
        qT = sb("qT", [P, G])
        rden = sb("rden", [P, SUB])
        full = sb("full", [P, 2 * SUB])
        rdf = sb("rdf", [P, SUB])
        empty = sb("empty", [P, 2 * SUB])
        y = sb("y", [P, SUB, D])
        stats = sb("stats", [P, SUB, 6])
        mv = sb("mv", [P, SUB, 2])
        mvs = sb("mvs", [P, NG * SUB, 2])
        rstd = sb("rstd", [P, NG * SUB])
        var = sb("var", [P, NG * SUB])
        half = sb("half", [P, NG * SUB], I32)
        rsq = sb("rsq", [P, NG * SUB])
        shifts = sb("shifts", [P, NG * SUB])
        xn = sb("xn", [P, SUB, D])
        xsum = sb("xsum", [P, NG])
        xmean = sb("xmean", [P, 1])
        hrow = sb("hrow", [P, SUB, HW])
        s1col = sb("s1col", [P, NG * SUB])

        ps_T = pb("ps_T", [P, U, P])
        ps_S = pb("ps_S", [P, U, 512])
        ps_O = pb("ps_O", [P, SUB, D + 1])
        ps_B = pb("ps_B", [P, G])
        ps_L = pb("ps_L", [P, 512])
        ps_X = pb("ps_X", [P, 512])

        s_load = sem("s_load")
        s_feat = sem("s_feat")
        s_ones = sem("s_ones")
        s_const = sem("s_const")
        s_vconst = sem("s_vconst")
        s_wx = sem("s_wx")
        s_w1x = sem("s_w1x")
        s_mean = sem("s_mean")
        s_meanc = sem("s_meanc")
        s_xmean = sem("s_xmean")
        s_scan = [sem(f"s_scan{b}") for b in range(RING)]
        s_piece_v = sem("s_piece_v")
        s_scan_a = sem("s_scan_a")
        s_occ_a = sem("s_occ_a")
        s_occ_free = sem("s_occ_free")
        s_tot = sem("s_tot")
        s_off = sem("s_off")
        s_bound = sem("s_bound")
        s_reach = sem("s_reach")
        s_pick = sem("s_pick")
        s_list = sem("s_list")
        s_small = sem("s_small")
        s_small_free = sem("s_small_free")
        s_apart = sem("s_apart")
        s_idx = sem("s_idx")
        s_gf = [sem(f"s_gf{u}") for u in range(U)]
        s_gm = [sem(f"s_gm{u}") for u in range(U)]
        s_feed = sem("s_feed")
        s_kst = sem("s_kst")
        s_tr = sem("s_tr")
        s_kt = sem("s_kt")
        s_fill = sem("s_fill")
        s_mst = sem("s_mst")
        s_raw = sem("s_raw")
        s_sc = sem("s_sc")
        s_max = sem("s_max")
        s_mT = sem("s_mT")
        s_diag = sem("s_diag")
        s_diag_flat = sem("s_diag_flat")
        s_flat = sem("s_flat")
        s_mb = sem("s_mb")
        s_dif = sem("s_dif")
        s_p = sem("s_p")
        s_pv = sem("s_pv")
        s_pre = sem("s_pre")
        s_q = sem("s_q")
        s_O = sem("s_O")
        s_O_free = sem("s_O_free")
        s_xn = sem("s_xn")
        s_xT = sem("s_xT")
        s_xTc = sem("s_xTc")
        s_h = sem("s_h")
        s_hc = sem("s_hc")
        s_st = sem("s_st")
        s_rstd = sem("s_rstd")
        s_norm = sem("s_norm")
        s_out = sem("s_out")

        feat_all = S[:, 0:C * D]
        xnT = qT
        diag_flat = xn
        y_all = scan_buf[:, :, :, :].rearrange("p b c i -> p (b c i)")[:, 0:NG * G].bitcast(F32)
        block = ctx.enter_context(nc.Block())

        def rounds(eng, layer, g):
            at = layer * (NG + 1)
            lo = eng.value_load(bounds[0:1, bass.ds(g + at, 1)], min_val=0, max_val=2 * NG * TURNS)
            hi = eng.value_load(bounds[0:1, bass.ds(g + at + 1, 1)], min_val=1, max_val=2 * NG * TURNS)
            return lo, hi

        @contextmanager
        def steps_of(eng, g):
            turn = eng.value_load(bounds[0:1, bass.ds(g, 1)], min_val=0, max_val=NG * TURNS)
            at = 2 * (NG + 1)
            lo = eng.value_load(bounds[0:1, bass.ds(g + at, 1)], min_val=0, max_val=NG * TURNS)
            hi = eng.value_load(bounds[0:1, bass.ds(g + at + 1, 1)], min_val=1, max_val=NG * TURNS)
            with eng.Fori(lo, hi) as j:
                yield j, nc.s_assert_within(
                    turn + (j - lo) * (W // U), 0, NG * TURNS - 1,
                    skip_runtime_bounds_check_because="a group has at most TURNS turns, TURNS even")

        def ring(eng, k):
            return eng.snap((k % TURNS) * U)

        def listed(eng, k, end=None):
            at = k if end is None else (k * -1) + (end - 1)
            return eng.snap(nc.s_assert_within(
                at, 0, NG * TURNS - 1, skip_runtime_bounds_check_because="a group has at most TURNS turns"))

        def backwards(eng, g):
            return eng.snap(nc.s_assert_within((g * -1) + (NG - 1), 0, NG - 1,
                                               skip_runtime_bounds_check_because="g runs to NG"))

        def apart(eng):
            eng.sem_inc(s_apart, 1)

        @block.sync
        def _(sp):
            def scan(g):
                for n in range(V_PIECES):
                    sp.wait_ge(s_piece_v, g * V_PIECES + n + 1)
                    sp.dma_start(scan_buf[:, n % RING, :, :],
                                 scan_src[bass.ds(g, 1), :, n * PC:(n + 1) * PC, :].rearrange("g p c i -> (g p) c i")
                                 ).then_inc(s_scan[n % RING], 16)

            def small(layer, g):
                if layer == 1:
                    sp.wait_ge(s_small, 32 * NG + 16 * g)
                elif not isinstance(g, int) or g > 0:
                    sp.wait_ge(s_small, 32 * g)
                apart(sp)
                sp.wait_ge(s_small_free, g + layer * NG + 1)
                apart(sp)
                at = bass.ds((g % 2) * G, G)
                if layer == 0:
                    sp.dma_start(xT_sb[:, at], xT_groups[bass.ds(g, 1), :, :].rearrange("g d i -> (g d) i")
                                 ).then_inc(s_small, 16)
                rows, group = (x_rows, g) if layer == 0 else (x1_rows, backwards(sp, g))
                sp.dma_start(xres[:, at].rearrange("p (s d) -> p s d", s=SUB),
                             rows[bass.ds(group, 1), :, :, :].rearrange("g p s d -> (g p) s d")).then_inc(s_small, 16)

            scan(0)
            sp.dma_start(w0_sb[:, :], w0).then_inc(s_load, 16)
            sp.dma_start(w1x[:, 0:D], w1).then_inc(s_load, 16)
            sp.dma_start(w1T_sb[:, :], w1T).then_inc(s_load, 16)
            sp.dma_start(a_sb[:, :], a).then_inc(s_load, 16)
            sp.dma_start(feat_all, feat.rearrange("(p c) d -> p (c d)", c=C)).then_inc(s_feat, 16)
            small(0, 0)
            for g in range(1, AHEAD):
                scan(g)
            with sp.Fori(0, NG - AHEAD) as g:
                small(0, sp.snap(g + 1))
                scan(sp.snap(g + AHEAD))
            for g in range(NG - AHEAD + 1, NG):
                small(0, g)
            sp.wait_ge(s_st, 32 * NG + 32)
            end = sp.value_load(bounds[0:1, 2 * NG + 1:2 * NG + 2], min_val=1, max_val=2 * NG * TURNS)
            with sp.Fori(0, NG) as g:
                lo, hi = rounds(sp, 1, g)
                with sp.Fori(lo, hi) as k:
                    sp.wait_ge(s_pv, k * U + U)
                    sp.wait_ge(s_mst, k * 16 + 16)
                    apart(sp)
                    sp.dma_start(F[:, bass.ds(ring(sp, k) * G, U * G)].rearrange("p (u i) -> p u i", u=U),
                                 masks[bass.ds(listed(sp, k, end), 1), :, :, :].rearrange("t p u i -> (t p) u i")
                                 ).then_inc(s_mst, 16)
                small(1, g)
            sp.wait_ge(s_out, 16 * NG)

        @block.gpsimd
        def _(pool):
            nc.gpsimd.memset(ones[:, :], 1.0).then_inc(s_ones, 1)
            nc.gpsimd.memset(onesC[:, :], 1.0)
            nc.gpsimd.memset(big[:, :], BIG)
            nc.gpsimd.memset(zrow[:, :], 0.0)
            nc.gpsimd.memset(hrow[:, :, DEN:DEN + 1], 1.0)
            nc.gpsimd.iota(iota_s[:, :], [[1, U * P]], base=0, channel_multiplier=0, allow_small_or_imprecise_dtypes=True)
            nc.gpsimd.iota(iota_turn[:, :], [[P * U, TURNS]], base=0, channel_multiplier=0,
                           allow_small_or_imprecise_dtypes=True)
            nc.gpsimd.iota(place_i[:, :], [[P, W]], base=0, channel_multiplier=1)
            nc.gpsimd.memset(group_row[:, :], float(-PADROW))
            nc.gpsimd.memset(V[:, :].rearrange("p (r w) -> p r w", w=HW)[:, :, DEN:DEN + 1], 1.0)
            pool.wait_ge(s_ones, 1)
            for target, base, op in ((ident, 0, ALU.is_equal), (before, 0, ALU.is_gt), (shift, -1, ALU.is_equal)):
                nc.gpsimd.affine_select(out=target[:, :], in_=ones[:, :], pattern=[[1, P]], compare_op=op,
                                        fill=0.0, base=base, channel_multiplier=-1)
            nc.gpsimd.affine_select(out=local[:, C:C + 1], in_=ones[:, 0:1], pattern=[[0, 1]], compare_op=ALU.is_gt,
                                    fill=0.0, base=0, channel_multiplier=1).then_inc(s_const, 1)

            def fetch(layer, k, end=None):
                at = listed(pool, k, end)
                for u in range(U):
                    pool.wait_ge(s_feed, k * U + u + 1)
                    apart(pool)
                    nc.gpsimd.tensor_copy(idx[:, u, :], lists[:, bass.ds(at * U + u, 1), :].rearrange("p o t -> p (o t)")
                                          ).then_inc(s_idx, 1)
                    pool.wait_ge(s_idx, k * U + u + 1)
                    apart(pool)
                    pool.indirect_dma_start(
                        out=st_feat[:, u, 0:(D if layer == 0 else HW)], out_offset=None,
                        in_=(feat if layer == 0 else table),
                        in_offset=bass.IndirectOffsetOnAxis(idx[:, u, 0:1].bitcast(U32), 0)).then_inc(s_gf[u], 16)
                    if layer == 0:
                        pool.indirect_dma_start(
                            out=st_mask[:, u, :], out_offset=None, in_=adjT,
                            in_offset=bass.IndirectOffsetOnAxis(idx[:, u, 1:2].bitcast(U32), 0)).then_inc(s_gm[u], 16)

            def feed(layer, k):
                slot = ring(pool, k)
                w = D if layer == 0 else HW
                for u in range(U):
                    pool.wait_ge(s_pv, k * U + u + 1)
                    pool.wait_ge(s_gf[u], 16 * k + 16)
                    apart(pool)
                    last = nc.gpsimd.tensor_copy(V[:, bass.ds((slot + u) * HW, w)], st_feat[:, u, 0:w])
                    if layer == 0:
                        pool.wait_ge(s_gm[u], 16 * k + 16)
                        apart(pool)
                        last = nc.gpsimd.tensor_copy(F[:, bass.ds((slot + u) * G, G)], st_mask[:, u, :])
                    last.then_inc(s_feed, 1)

            pool.sem_inc(s_feed, U)
            with pool.Fori(0, NG) as g:
                pool.wait_ge(s_list, g + 1)
                apart(pool)
                lo, hi = rounds(pool, 0, g)
                with pool.Fori(lo, hi) as k:
                    fetch(0, k)
                    feed(0, k)
            pool.wait_ge(s_st, 32 * NG + 32)
            total = pool.value_load(bounds[0:1, NG:NG + 1], min_val=1, max_val=NG * TURNS)
            end = pool.value_load(bounds[0:1, 2 * NG + 1:2 * NG + 2], min_val=1, max_val=2 * NG * TURNS)
            with pool.Fori(total, end) as k:
                fetch(1, k, end)
                feed(1, k)

        @block.scalar
        def _(act):
            act.sem_inc(s_mst, 16)
            act.sem_inc(s_st, 32)
            def load_piece(g, n):
                act.dma_start(scan_buf[:, RING, :, :],
                              scan_src[bass.ds(g, 1), :, n * PC:(n + 1) * PC, :].rearrange("g p c i -> (g p) c i")
                              ).then_inc(s_scan_a, 16)

            load_piece(0, V_PIECES)
            def weights():
                act.wait_ge(s_wx, 1)
                nc.scalar.copy(w1x[:, COLT:COLT + 1], ps_X[:, 1:2])
                nc.scalar.mul(w1x[:, COLTS:COLTS + 1], ps_X[:, 1:2], SLOPE)
                nc.scalar.copy(w1x[:, ROWT:ROWT + 1], ps_X[:, 0:1]).then_inc(s_w1x, 1)
                act.wait_ge(s_mean, 1)
                nc.scalar.mul(mean0[:, :], ps_X[:, 0:D], 1.0 / N).then_inc(s_meanc, 1)

            def scan(g, stage, load_next=True):
                if stage == 0:
                    act.wait_ge(s_occ_free, g + 1)
                for n in range(*A_STAGES[stage]):
                    done = g * A_PIECES + n - V_PIECES
                    act.wait_ge(s_scan_a, done * 16 + 16)
                    for c in range(PC):
                        last = nc.scalar.activation(scan_buf[:, RING, c, :], scan_buf[:, RING, c, :], ACT.Relu,
                                                    accum_out=occ[:, n * PC + c:n * PC + c + 1])
                    last.then_inc(s_occ_a, 1)
                    if load_next:
                        act.wait_ge(s_occ_a, done + 1)
                        apart(act)
                        if n < PIECES - 1:
                            load_piece(g, n + 1)
                        else:
                            load_piece(g + 1, V_PIECES)

            def exponentials(lo, hi, scale):
                with act.Fori(lo, hi) as k:
                    slot = ring(act, k)
                    act.wait_ge(s_dif, k + 2)
                    for u in range(U):
                        act.wait_ge(s_pv, k * U + u + 1 + C - U)
                        nc.scalar.activation(prob[:, u, :], S[:, bass.ds((slot + u) * G, G)], ACT.Exp,
                                             scale=scale).then_inc(s_p, 1)

            def queries(g):
                act.wait_ge(s_pre, g + 1)
                nc.scalar.copy(qT[:, :], ps_L[:, 0:G]).then_inc(s_q, 1)

            def listed_rounds(g):
                act.wait_ge(s_list, g + 1)
                apart(act)
                return rounds(act, 0, g)

            def scores(lo, hi):
                with act.Fori(lo, hi) as k:
                    slot = ring(act, k)
                    at = listed(act, k)
                    act.wait_ge(s_feed, k * U + 2 * U)
                    nc.scalar.copy(kst[:, :, :],
                                   V[:, bass.ds(slot * HW, U * HW)].rearrange("p (u w) -> p u w", u=U)[:, :, 0:D]
                                   ).then_inc(s_kst, 1)
                    act.wait_ge(s_tr, k + 1)
                    nc.scalar.copy(kT[:, :, :], ps_T[:, :, :]).then_inc(s_kt, 1)
                    act.wait_ge(s_mst, 16 * k + 16)
                    nc.scalar.activation(fill[:, :, :], F[:, bass.ds(slot * G, U * G)].rearrange("p (u i) -> p u i", u=U),
                                         ACT.Relu, scale=-BIG, bias=big[:, 0:1]).then_inc(s_fill, 1)
                    act.wait_ge(s_fill, k + 1)
                    act.dma_start(masks[bass.ds(at, 1), :, :, :].rearrange("t p u i -> (t p) u i"),
                                  fill[:, :, :]).then_inc(s_mst, 16)
                    for u in range(U):
                        act.wait_ge(s_raw, k * U + u + 1)
                        nc.scalar.copy(S[:, bass.ds((slot + u) * G, G)], ps_S[:, u, 0:G]).then_inc(s_sc, 1)

            def new_rows(g):
                act.wait_ge(s_xT, g + 1)
                nc.scalar.activation(xnT[:, :], ps_X[:, 0:G], ACT.Copy,
                                     accum_out=xsum[:, bass.ds(g, 1)]).then_inc(s_xTc, 1)
                act.wait_ge(s_h, g + 1)
                act.wait_ge(s_st, 32 * g + 32)
                hx = ps_X[:, 0:SUB * WX].rearrange("p (s w) -> p s w", s=SUB)
                nc.scalar.copy(hrow[:, :, 0:D], hx[:, :, 0:D])
                nc.scalar.copy(hrow[:, :, COLT:HW], hx[:, :, COLT:HW])
                nc.scalar.copy(s1col[:, bass.ds(g * SUB, SUB)], hx[:, :, ROWT:WX].rearrange("p s o -> p (s o)")
                               ).then_inc(s_hc, 1)
                act.wait_ge(s_hc, g + 1)
                act.dma_start(table_rows[bass.ds(g, 1), :, :, :].rearrange("g p s d -> (g p) s d"),
                              hrow[:, :, :]).then_inc(s_st, 16)
                act.dma_start(x1_rows[bass.ds(g, 1), :, :, :].rearrange("g p s d -> (g p) s d"),
                              xn[:, :, :]).then_inc(s_st, 16)

            def attend1(g):
                lo, hi = rounds(act, 1, g)
                act.wait_ge(s_flat, g + 1)
                with act.Fori(lo, hi) as k:
                    slot = ring(act, k)
                    for u in range(U):
                        nc.scalar.activation(S[:, bass.ds((slot + u) * G, G)], ps_S[:, 0, 0:G], ACT.Identity,
                                             bias=V[:, bass.ds((slot + u) * HW + COLTS, 1)]).then_inc(s_sc, 1)
                exponentials(lo, hi, 1.0)

            def attend0(g, scans, scores_next, first=False, last=False):
                lo, hi = rounds(act, 0, g)
                if scores_next:
                    lo_next, hi_next = listed_rounds(g + 1)
                if not first:
                    new_rows(g - 1)
                if scans:
                    scan(g + AHEAD, 0)
                if scores_next:
                    queries(g + 1)
                exponentials(lo, hi, 1.0 / TEMPERATURE)
                if scans:
                    scan(g + AHEAD, 1)
                if scores_next:
                    scores(lo_next, hi_next)
                if scans:
                    scan(g + AHEAD, 2, load_next=not last)

            for g in range(AHEAD):
                if g == AHEAD - 1:
                    weights()
                    queries(0)
                    scores(*listed_rounds(0))
                for stage in range(len(A_STAGES)):
                    scan(g, stage)
            attend0(0, True, True, first=True)
            with act.Fori(1, NG - AHEAD - 1) as g:
                attend0(g, True, True)
            attend0(NG - AHEAD - 1, True, True, last=True)
            with act.Fori(NG - AHEAD, NG - 1) as g:
                attend0(g, False, True)
            attend0(NG - 1, False, False)
            new_rows(NG - 1)
            act.wait_ge(s_mean, 2)
            nc.scalar.copy(mean1[:, :], ps_X[:, 0:D]).then_inc(s_meanc, 1)

            def store_output(g):
                act.dma_start(out_rows[NG - 1 - g], y_all[:, g * G:(g + 1) * G].rearrange("p (s d) -> p s d", s=SUB)
                              ).then_inc(s_out, 16)

            with act.Fori(0, NG - 1) as g:
                attend1(g)
            act.wait_ge(s_rstd, 1)
            for g in range(NG - LATE):
                for n in range(g * SUB, (g + 1) * SUB):
                    rows = y_all[:, n * D:(n + 1) * D]
                    last = nc.scalar.activation(rows, rows, ACT.Identity, scale=rstd[:, n:n + 1], bias=shifts[:, n:n + 1])
                last.then_inc(s_norm, 1)
                act.wait_ge(s_norm, g + 1)
                store_output(g)
            attend1(NG - 1)
            for g in range(NG - LATE, NG):
                act.wait_ge(s_xn, g + LATE + 1)
                store_output(g)
            act.wait_ge(s_out, 16 * NG)

        @block.tensor
        def _(pe):
            pe.sem_inc(s_pv, C)
            pe.wait_ge(s_const, 1)
            def compact(g):
                pe.wait_ge(s_tot, g + 1)
                count = prefix[:, C - 1:C]
                nc.tensor.matmul(ps_L[:, 0:C], steps[:, :], prefix[:, :], start=True, stop=True)
                nc.tensor.matmul(ps_L[:, C:C + 1], shift[:, :], count, start=True, stop=True)
                nc.tensor.matmul(ps_L[:, C + 1:C + 2], before[:, :], count, start=True, stop=True)
                nc.tensor.matmul(ps_L[:, C + 2:C + 3], ones[:, :], count, start=True, stop=True).then_inc(s_off, 1)
                pe.wait_ge(s_bound, g + 1)
                apart(pe)
                with steps_of(pe, g) as (j, _):
                    pe.wait_ge(s_reach, j + 1)
                    for u in range(W):
                        last = nc.tensor.matmul(ps_L[:, 64 * (u + 1):64 * (u + 1) + LOC],
                                                reached[:, u * P:(u + 1) * P], local[:, :], start=True, stop=True)
                    last.then_inc(s_pick, 1)

            def transpose_maximum(gg):
                pe.wait_ge(s_max, gg + 1)
                for s in range(SUB):
                    last = nc.tensor.transpose(ps_B[:, s * P:(s + 1) * P], M[:, s * P:(s + 1) * P], ident[:, :])
                last.then_inc(s_mT, 1)

            def zero_sums(gg):
                pe.wait_ge(s_O_free, gg + 1)
                nc.tensor.matmul(ps_O[:, :, :].rearrange("p s d -> p (s d)"), zrow[:, 0:P], zrow[:, 0:SUB * (D + 1)],
                                 start=True, stop=False, skip_group_check=True)

            def broadcast(layer, gg):
                if layer == 1:
                    pe.wait_ge(s_diag_flat, gg - NG + 1)
                    nc.tensor.matmul(ps_S[:, 0, 0:G], ones[:, :], diag_flat[:, :, :].rearrange("p s i -> p (s i)"),
                                     start=True, stop=True).then_inc(s_flat, 1)
                pe.wait_ge(s_diag, gg + 1)
                nc.tensor.matmul(ps_B[:, :], ones[:, :], diag[:, :, :].rearrange("p s i -> p (s i)"),
                                 start=True, stop=True).then_inc(s_mb, 1)

            def sums(lo, hi):
                with pe.Fori(lo, hi) as k:
                    slot = ring(pe, k)
                    for u in range(U):
                        pe.wait_ge(s_p, k * U + u + 1)
                        for s in range(SUB):
                            last = nc.tensor.matmul(ps_O[:, s, :], prob[:, u, s * P:(s + 1) * P],
                                                    V[:, bass.ds((slot + u) * HW, D + 1)], start=False, stop=False,
                                                    skip_group_check=True)
                        last.then_inc(s_pv, 1)
                nc.tensor.matmul(ps_O[:, :, :].rearrange("p s d -> p (s d)"), zrow[:, 0:P], zrow[:, 0:SUB * (D + 1)],
                                 start=False, stop=True, skip_group_check=True).then_inc(s_O, 1)

            def queries(g, lists_done):
                pe.wait_ge(s_list, lists_done)
                pe.wait_ge(s_small, 32 * g + 32)
                nc.tensor.matmul(ps_L[:, 0:G], w0_sb[:, :], xT_sb[:, bass.ds((g % 2) * G, G)],
                                 start=True, stop=True).then_inc(s_pre, 1)

            def scores(g, lo, hi):
                pe.wait_ge(s_q, g + 1)
                apart(pe)
                with pe.Fori(lo, hi) as k:
                    pe.wait_ge(s_kst, k + 1)
                    for u in range(U):
                        last = nc.tensor.transpose(ps_T[:, u, :], kst[:, u, :], ident[:, :])
                    last.then_inc(s_tr, 1)
                    pe.wait_ge(s_kt, k + 1)
                    for u in range(U + 1):
                        if u < U:
                            nc.tensor.matmul(ps_S[:, u, 0:G], kT[:, u, :], qT[:, :], start=True, stop=False)
                        if u == 1:
                            pe.wait_ge(s_fill, k + 1)
                        if u > 0:
                            nc.tensor.matmul(ps_S[:, u - 1, 0:G], mask_w[:, :], fill[:, u - 1, :], start=False, stop=True
                                             ).then_inc(s_raw, 1)

            def new_rows(g):
                pe.wait_ge(s_xn, g + 1)
                for s in range(SUB):
                    last = nc.tensor.transpose(ps_X[:, s * P:(s + 1) * P], xn[:, s, :], ident[:, :])
                last.then_inc(s_xT, 1)
                pe.wait_ge(s_xTc, g + 1)
                for s in range(SUB):
                    last = nc.tensor.matmul(ps_X[:, s * WX:(s + 1) * WX], xnT[:, s * P:(s + 1) * P], w1x[:, :],
                                            start=(s == 0), stop=True, skip_group_check=True)
                last.then_inc(s_h, 1)

            def attend0(g, compacts, scores_next):
                zero_sums(g)
                broadcast(0, g)
                if scores_next:
                    queries(g + 1, g + AHEAD if compacts else NG)
                    lo_next, hi_next = rounds(pe, 0, g + 1)
                sums(*rounds(pe, 0, g))
                if scores_next:
                    scores(g + 1, lo_next, hi_next)
                if scores_next:
                    transpose_maximum(g + 1)
                if compacts:
                    compact(g + AHEAD)
                new_rows(g)

            def attend1(g):
                transpose_maximum(g + NG)
                broadcast(1, g + NG)
                zero_sums(g + NG)
                sums(*rounds(pe, 1, g))

            pe.wait_ge(s_vconst, 1)
            for g in range(AHEAD - 1):
                compact(g)
            pe.wait_ge(s_load, 64)
            nc.tensor.matmul(ps_X[:, 0:2], w1T_sb[:, :], a_sb[:, :], start=True, stop=True).then_inc(s_wx, 1)
            pe.wait_ge(s_w1x, 1)
            pe.wait_ge(s_feat, 16)
            for c in range(C):
                last = nc.tensor.matmul(ps_X[:, 0:D], ones[:, :], feat_all[:, c * D:(c + 1) * D],
                                        start=(c == 0), stop=(c == C - 1))
            last.then_inc(s_mean, 1)
            pe.wait_ge(s_meanc, 1)
            queries(0, AHEAD - 1)
            scores(0, *rounds(pe, 0, 0))
            transpose_maximum(0)
            compact(AHEAD - 1)
            with pe.Fori(0, NG - AHEAD) as g:
                attend0(g, True, True)
            with pe.Fori(NG - AHEAD, NG - 1) as g:
                attend0(g, False, True)
            attend0(NG - 1, False, False)
            pe.wait_ge(s_hc, NG)
            pe.wait_ge(s_xmean, 1)
            nc.tensor.matmul(ps_X[:, 0:D], diag[:, 0, :], w1x[:, 0:D], start=True, stop=True).then_inc(s_mean, 1)
            with pe.Fori(0, NG) as g:
                attend1(g)

        @block.vector
        def _(dve):
            dve.sem_inc(s_piece_v, RING)
            dve.sem_inc(s_occ_free, 1)
            dve.sem_inc(s_small_free, 2)
            dve.sem_inc(s_O_free, 1)
            dve.sem_inc(s_dif, 1)
            nc.vector.memset(turn_sum[:, :], 0.0)
            nc.vector.memset(bounds[:, :], 0)
            nc.vector.memset(w1x[:, DEN:DEN + 1], 0.0)
            dve.wait_ge(s_const, 1)
            nc.vector.tensor_tensor(steps[:, :], ident[:, :], shift[:, :], ALU.subtract)
            nc.vector.tensor_scalar(mask_w[:, :], ident[:, :], -1.0, None, ALU.mult).then_inc(s_vconst, 1)

            def scan(g, stage):
                for n in range(*V_STAGES[stage]):
                    dve.wait_ge(s_scan[n % RING], (g * PER_RING + n // RING) * 16 + 16)
                    nc.vector.tensor_reduce(occ[:, n * PC:(n + 1) * PC], scan_buf[:, n % RING, :, :],
                                            AX.X, ALU.max).then_inc(s_piece_v, 1)

            def compact(g, scans=True):
                dve.drain()
                dve.wait_ge(s_occ_a, g * A_PIECES + A_PIECES)
                nc.vector.tensor_scalar(present[:, :], occ[:, :], 0.0, None, ALU.is_gt).then_inc(s_occ_free, 1)
                dve.drain()
                nc.vector.tensor_tensor_scan(prefix[:, :], onesC[:, :], present[:, :], 0.0, ALU.mult, ALU.add
                                             ).then_inc(s_tot, 1)
                nc.vector.tensor_copy(place[:, :], place0[:, :])
                if scans:
                    scan(g + 1, 0)
                dve.wait_ge(s_off, g + 1)
                nc.vector.tensor_copy(offs[:, :], ps_L[:, C + 1:C + 3])
                nc.vector.tensor_copy(local[:, 0:C], ps_L[:, 0:C])
                nc.vector.tensor_copy(local[:, C + 1:C + 2], ps_L[:, C:C + 1])
                dve.drain()
                nc.vector.tensor_scalar(turn_flags[:, :], iota_turn[:, :], offs[0:1, 1:2], None, ALU.is_lt)
                nc.vector.tensor_copy(first[:, :], offs[:, 0:1])
                dve.drain()
                nc.vector.tensor_reduce(turn_n[:, 0:1], turn_flags[:, :], AX.X, ALU.add)
                nc.vector.tensor_reduce(turn_n[:, 1:2],
                                        turn_flags[:, :].rearrange("o (j t) -> o t j", t=W // U)[:, 0:1, :],
                                        AX.X, ALU.add)
                dve.drain()
                nc.vector.scalar_tensor_tensor(out=turn_sum[:, :], in0=turn_n[:, :], scalar=1.0,
                                               in1=turn_sum[:, :], op0=ALU.max, op1=ALU.add)
                dve.drain()
                nc.vector.tensor_copy(bounds[0:1, bass.ds(g + 1, 1)], turn_sum[:, 0:1])
                nc.vector.tensor_scalar(bounds[0:1, bass.ds((g * -1) + 2 * NG, 1)], turn_sum[:, 0:1], -1.0, None, ALU.mult)
                nc.vector.tensor_copy(bounds[0:1, bass.ds(g + 1 + 2 * (NG + 1), 1)], turn_sum[:, 1:2]
                                      ).then_inc(s_bound, 1)
                if scans:
                    scan(g + 1, 1)
                dve.wait_ge(s_bound, g + 1)
                apart(dve)
                with steps_of(dve, g) as (j, turn):
                    at = dve.snap(turn * U)
                    nc.vector.tensor_scalar(reached[:, 0:U * P], iota_s[:, :], first[:, 0:1], None, ALU.is_ge)
                    nc.vector.tensor_scalar(reached[:, U * P:W * P], iota_s[:, :], float(U * P), first[:, 0:1],
                                            ALU.add, ALU.is_ge).then_inc(s_reach, 1)
                    nc.vector.tensor_scalar(real[:, :], place[:, :], offs[:, 1:2], None, ALU.is_lt)
                    nc.vector.tensor_scalar(first[:, :], first[:, :], float(-W * P), None, ALU.add)
                    dve.wait_ge(s_pick, j + 1)
                    pick = ps_L[:, 64:64 * (W + 1)].rearrange("p (u w) -> p u w", u=W)
                    nc.vector.tensor_tensor(rank[:, :], place[:, :], pick[:, :, C + 1:C + 2].rearrange("p u o -> p (u o)"),
                                            ALU.subtract)
                    dve.drain()
                    nc.vector.tensor_tensor(ahead[:, :, :], pick[:, :, 0:C],
                                            rank[:, :].unsqueeze(2).to_broadcast([P, W, C]), ALU.is_le)
                    nc.vector.tensor_scalar(place[:, :], place[:, :], float(W * P), None, ALU.add)
                    dve.drain()
                    nc.vector.tensor_reduce(ccol[:, :], ahead[:, :, :], AX.X, ALU.add)
                    dve.drain()
                    nc.vector.scalar_tensor_tensor(out=jcol[:, :], in0=pick[:, :, C:C + 1].rearrange("p u o -> p (u o)"),
                                                   scalar=float(C), in1=ccol[:, :], op0=ALU.mult, op1=ALU.add)
                    dve.drain()
                    nc.vector.scalar_tensor_tensor(out=mrow[:, :], in0=jcol[:, :], scalar=group_row[:, 0:1],
                                                   in1=real[:, :], op0=ALU.add, op1=ALU.mult)
                    nc.vector.tensor_scalar(lists[:, bass.ds(at, W), 0], jcol[:, :], float(N - 1), None, ALU.min)
                    dve.drain()
                    nc.vector.tensor_scalar(lists[:, bass.ds(at, W), 1], mrow[:, :], float(PADROW), None, ALU.add)
                dve.drain()
                nc.vector.tensor_scalar(group_row[:, :], group_row[:, :], float(N), None, ALU.add
                                        ).then_inc(s_list, 1)

            def rsqrt(n):
                dve.drain()
                nc.vector.tensor_scalar(half[:, 0:n], var[:, 0:n].bitcast(I32), 1, None, ALU.logical_shift_right)
                dve.drain()
                nc.vector.tensor_scalar(rstd[:, 0:n].bitcast(I32), half[:, 0:n], -1.0, float(0x5F3759DF),
                                        ALU.mult, ALU.add)
                for _ in range(3):
                    dve.drain()
                    nc.vector.tensor_tensor(rsq[:, 0:n], rstd[:, 0:n], rstd[:, 0:n], ALU.mult)
                    dve.drain()
                    nc.vector.scalar_tensor_tensor(out=rsq[:, 0:n], in0=rsq[:, 0:n], scalar=-0.5, in1=var[:, 0:n],
                                                   op0=ALU.mult, op1=ALU.mult)
                    dve.drain()
                    nc.vector.scalar_tensor_tensor(out=rstd[:, 0:n], in0=rsq[:, 0:n], scalar=1.5, in1=rstd[:, 0:n],
                                                   op0=ALU.add, op1=ALU.mult)
                dve.drain()

            def diagonal(target, col):
                return nc.vector.tensor_tensor(target[:, :, :], ident[:, :].unsqueeze(1).to_broadcast([P, SUB, P]),
                                               col.unsqueeze(2).to_broadcast([P, SUB, P]), ALU.mult)

            def attended(layer, g, target):
                dve.wait_ge(s_O, g + layer * NG + 1)
                nc.vector.tensor_scalar(rden[:, :], ps_O[:, :, DEN:DEN + 1].rearrange("p s o -> p (s o)"), 0.5, None,
                                        ALU.max)
                dve.drain()
                nc.vector.reciprocal(rden[:, :], rden[:, :])
                dve.drain()
                nc.vector.tensor_tensor(rdf[:, :], rden[:, :], full[:, bass.ds((g % 2) * SUB, SUB)], ALU.mult)
                dve.drain()
                if layer == 0:
                    dve.wait_ge(s_small, 32 * g + 32)
                else:
                    dve.wait_ge(s_small, 32 * NG + 16 * g + 16)
                    dve.wait_ge(s_meanc, 2)
                for s in range(SUB):
                    last = nc.vector.scalar_tensor_tensor(out=y[:, s, :], in0=ps_O[:, s, 0:D], scalar=rdf[:, s:s + 1],
                                                          in1=xres[:, bass.ds((g % 2) * G + s * D, D)],
                                                          op0=ALU.mult, op1=ALU.add)
                last.then_inc(s_small_free, 1)
                dve.drain()
                for s in range(SUB):
                    last = nc.vector.scalar_tensor_tensor(out=target(s), in0=(mean0 if layer == 0 else mean1)[:, :],
                                                          scalar=empty[:, bass.ds((g % 2) * SUB + s, 1)], in1=y[:, s, :],
                                                          op0=ALU.mult, op1=ALU.add)
                last.then_inc(s_O_free, 1)
                dve.drain()
                for s in range(SUB):
                    nc.vector.bn_stats(stats[:, s, :], target(s))
                dve.drain()
                for s in range(SUB):
                    nc.vector.bn_aggr(mv[:, s, :], stats[:, s, :])
                dve.drain()

            def maximum_ready():
                dve.drain()
                nc.vector.tensor_copy(mcol[:, 0:1], M[:, 0:1]).then_inc(s_max, 1)

            def row_maximum(layer, g):
                dve.wait_ge(s_mT, g + layer * NG + 1)
                nc.vector.tensor_reduce(mcol[:, :], ps_B[:, :].rearrange("p (s q) -> p s q", s=SUB), AX.X,
                                        ALU.max if layer == 0 else ALU.min)
                dve.drain()

            def greatest_scores(g):
                pair = y[:, :, :].rearrange("p s d -> p (s d)")
                lo, hi = rounds(dve, 0, g)
                dve.drain()
                nc.vector.memset(M[:, :], LEAST)
                with dve.Fori(lo, hi) as k:
                    slot = ring(dve, k)
                    dve.wait_ge(s_sc, k * U + 2)
                    nc.vector.tensor_tensor(pair, S[:, bass.ds(slot * G, G)], S[:, bass.ds((slot + 1) * G, G)], ALU.max)
                    dve.drain()
                    nc.vector.tensor_tensor(M[:, :], M[:, :], pair, ALU.max)
                    dve.drain()
                    dve.wait_ge(s_sc, k * U + 3)
                    nc.vector.tensor_tensor(M[:, :], M[:, :], S[:, bass.ds((slot + 2) * G, G)], ALU.max)
                maximum_ready()

            def attend0(g, scans, scores_next, final=False):
                row_maximum(0, g)
                diagonal(diag, mcol[:, :]).then_inc(s_diag, 1)
                nc.vector.tensor_scalar(empty[:, bass.ds((g % 2) * SUB, SUB)], mcol[:, :], -BIG / 2, None, ALU.is_lt)
                nc.vector.tensor_scalar(full[:, bass.ds((g % 2) * SUB, SUB)], mcol[:, :], -BIG / 2, None, ALU.is_ge)
                if scans:
                    scan(g + AHEAD, 2)
                lo, hi = rounds(dve, 0, g)
                dve.wait_ge(s_mb, g + 1)
                apart(dve)
                with dve.Fori(lo, hi) as k:
                    turn = S[:, bass.ds(ring(dve, k) * G, U * G)].rearrange("p (u i) -> p u i", u=U)
                    nc.vector.tensor_tensor(turn, turn, ps_B[:, :].unsqueeze(1).to_broadcast([P, U, G]), ALU.subtract
                                            ).then_inc(s_dif, 1)
                if scans:
                    scan(g + AHEAD, 3)
                attended(0, g, lambda s: y[:, s, :])
                nc.vector.tensor_scalar(var[:, 0:SUB], mv[:, :, 1:2].rearrange("p s o -> p (s o)"), EPS, None, ALU.add)
                rsqrt(SUB)
                dve.wait_ge(s_st, 32 * g + 32)
                for s in range(SUB):
                    last = nc.vector.tensor_scalar(xn[:, s, :], y[:, s, :], mv[:, s, 0:1], rstd[:, s:s + 1],
                                                   ALU.subtract, ALU.mult)
                last.then_inc(s_xn, 1)
                if scans:
                    scan(g + AHEAD, 4)
                if scores_next:
                    greatest_scores(g + 1)
                if scans:
                    compact(g + AHEAD, not final)

            def greatest_terms(lo, hi):
                nc.vector.memset(M[:, :], -LEAST)
                with dve.Fori(lo, hi) as k:
                    slot = ring(dve, k)
                    for u in range(U):
                        dve.drain()
                        if u == 0:
                            dve.wait_ge(s_mst, k * 16 + 32)
                            dve.wait_ge(s_feed, k * U + 2 * U)
                        nc.vector.scalar_tensor_tensor(out=M[:, :], in0=F[:, bass.ds((slot + u) * G, G)],
                                                       scalar=V[:, bass.ds((slot + u) * HW + COLT, 1)],
                                                       in1=M[:, :], op0=ALU.subtract, op1=ALU.min)
                maximum_ready()

            def row_terms(g):
                mine = bass.ds((g % 2) * SUB, SUB)
                row_maximum(1, g)
                s1 = s1col[:, bass.ds(backwards(dve, g) * SUB, SUB)]
                nc.vector.tensor_tensor(mrow_t[:, :], s1, mcol[:, :], ALU.subtract)
                nc.vector.tensor_scalar(empty[:, mine], mcol[:, :], BIG / 2, None, ALU.is_gt)
                nc.vector.tensor_scalar(full[:, mine], mcol[:, :], BIG / 2, None, ALU.is_le)
                dve.drain()
                nc.vector.scalar_tensor_tensor(out=mrow_t[:, :], in0=mrow_t[:, :], scalar=SLOPE, in1=mrow_t[:, :],
                                               op0=ALU.mult, op1=ALU.max)
                dve.drain()
                nc.vector.tensor_tensor(rterm[:, 0, :], s1, mrow_t[:, :], ALU.subtract)
                nc.vector.scalar_tensor_tensor(out=rterm[:, 1, :], in0=s1, scalar=SLOPE, in1=mrow_t[:, :],
                                               op0=ALU.mult, op1=ALU.subtract)
                dve.drain()
                diagonal(diag_flat, rterm[:, 1, :]).then_inc(s_diag_flat, 1)
                diagonal(diag, rterm[:, 0, :]).then_inc(s_diag, 1)

            def exponents1(g, lo, hi):
                dve.wait_ge(s_mb, g + NG + 1)
                apart(dve)
                with dve.Fori(lo, hi) as k:
                    slot = ring(dve, k)
                    for u in range(U):
                        dve.wait_ge(s_sc, k * U + u + 1)
                        at = bass.ds((slot + u) * G, G)
                        nc.vector.scalar_tensor_tensor(out=S[:, at], in0=ps_B[:, :],
                                                       scalar=V[:, bass.ds((slot + u) * HW + COLT, 1)],
                                                       in1=S[:, at], op0=ALU.add, op1=ALU.max)
                    dve.drain()
                    turn = bass.ds(slot * G, U * G)
                    nc.vector.tensor_tensor(S[:, turn], S[:, turn], F[:, turn], ALU.subtract).then_inc(s_dif, 1)

            def new_rows1(g):
                attended(1, g, lambda s: y_all[:, bass.ds(g * G + s * D, D)])
                nc.vector.tensor_copy(mvs[:, bass.ds(g * SUB, SUB), :], mv[:, :, :])

            nc.vector.tensor_copy(place0[:, :], place_i[:, :])
            dve.drain()
            for g in range(AHEAD):
                for stage in range(0 if g == 0 else 2, len(V_STAGES)):
                    scan(g, stage)
                if g == AHEAD - 1:
                    greatest_scores(0)
                compact(g)
            with dve.Fori(0, NG - AHEAD - 1) as g:
                attend0(g, True, True)
            attend0(NG - AHEAD - 1, True, True, final=True)
            with dve.Fori(NG - AHEAD, NG - 1) as g:
                attend0(g, False, True)
            nc.vector.tensor_scalar(bounds[0:1, NG + 1:2 * NG + 2], bounds[0:1, NG + 1:2 * NG + 2], turn_sum[0:1, 0:1],
                                    turn_sum[0:1, 0:1], ALU.add, ALU.add)
            attend0(NG - 1, False, False)
            dve.wait_ge(s_xTc, NG)
            nc.vector.tensor_reduce(xmean[:, :], xsum[:, :], AX.X, ALU.add)
            dve.drain()
            nc.vector.tensor_scalar(diag[:, 0, :], ones[:, :], xmean[:, 0:1], 1.0 / N, ALU.mult, ALU.mult
                                    ).then_inc(s_xmean, 1)
            dve.wait_ge(s_meanc, 2)
            lo, hi = rounds(dve, 1, 0)
            greatest_terms(lo, hi)
            row_terms(0)
            exponents1(0, lo, hi)
            def middle(g):
                lo, hi = rounds(dve, 1, g)
                greatest_terms(lo, hi)
                row_terms(g)
                new_rows1(g - 1)
                exponents1(g, lo, hi)

            def rstds(first, count):
                dve.drain()
                nc.vector.tensor_scalar(var[:, 0:count], mvs[:, first:first + count, 1:2].rearrange("p s o -> p (s o)"),
                                        EPS, None, ALU.add)
                rsqrt(count)

            with dve.Fori(1, NG - 1) as g:
                middle(g)
            early = (NG - LATE) * SUB
            rstds(0, early)
            nc.vector.scalar_tensor_tensor(out=shifts[:, 0:early], in0=mvs[:, 0:early, 0:1].rearrange("p s o -> p (s o)"),
                                           scalar=-1.0, in1=rstd[:, 0:early], op0=ALU.mult, op1=ALU.mult
                                           ).then_inc(s_rstd, 1)
            middle(NG - 1)
            new_rows1(NG - 1)
            dve.wait_ge(s_norm, NG - LATE)
            rstds(early, LATE * SUB)
            for g in range(NG - LATE, NG):
                for n in range(g * SUB, (g + 1) * SUB):
                    rows = y_all[:, n * D:(n + 1) * D]
                    last = nc.vector.tensor_scalar(rows, rows, mvs[:, n, 0:1], rstd[:, n - early:n - early + 1],
                                                   ALU.subtract, ALU.mult)
                last.then_inc(s_xn, 1)


def kernel(**inputs):
    import numpy as np
    import concourse.bacc as bacc
    from concourse import mybir as mb
    from concourse.bass_utils import run_bass_kernel_spmd

    x = np.ascontiguousarray(inputs["x"])
    adj = np.asarray(inputs["adj"])
    n, d = x.shape
    arrays = {
        "x": x,
        "xT": np.ascontiguousarray(x.T),
        "adjT": np.concatenate([adj.reshape(n // G, G, n).transpose(0, 2, 1).reshape(-1, G),
                                np.zeros((1, G), adj.dtype)]),
        "feat": np.ascontiguousarray(inputs["L0_gnn_input"]),
        "w0": np.ascontiguousarray(inputs["L0_gnn_weight"]),
        "w1": np.ascontiguousarray(inputs["L1_gnn_W"]),
        "w1T": np.ascontiguousarray(np.asarray(inputs["L1_gnn_W"]).T),
        "a": np.ascontiguousarray(np.asarray(inputs["L1_gnn_a"]).reshape(2, d).T),
    }
    nc = bacc.Bacc("TRN2", target_bir_lowering=False, num_devices=1)
    args = [nc.dram_tensor(f"in_{k}", v.shape, mb.dt.from_np(v.dtype), kind="ExternalInput").ap()
            for k, v in arrays.items()]
    x1_dram = nc.dram_tensor("x1_dram", (n, d), F32, kind="Internal").ap()
    table = nc.dram_tensor("table", (n, d + 3), F32, kind="Internal").ap()
    masks = nc.dram_tensor("masks", (n // G * (n // P // U), P, U, G), BF16, kind="Internal").ap()
    out = nc.dram_tensor("out_x", (n, d), F32, kind="ExternalOutput").ap()
    graph_attention_kernel(nc, *args, x1_dram, table, masks, out)
    r = run_bass_kernel_spmd(nc, [{f"in_{k}": v for k, v in arrays.items()}], core_ids=[0])
    return r.results[0]["out_x"]
```
